# Optimizing a Trainium2 kernel written in Bass

```python
import numpy as np
import jax
import jax.numpy as jnp

def _softmax(x, axis=-1):
    return jax.nn.softmax(x, axis=axis)

def _gelu(x):
    return jax.nn.gelu(x, approximate=True)

def _silu(x):
    return jax.nn.silu(x)

def _sigmoid(x):
    return jax.nn.sigmoid(x)

def _layernorm(x, axis=-1, eps=1e-05):
    m = jnp.mean(x, axis=axis, keepdims=True)
    v = jnp.var(x, axis=axis, keepdims=True)
    return (x - m) / jnp.sqrt(v + eps)

def _scatter_add(tgt, idx, src, axis=0):
    return tgt.at[idx].add(src)

def _segment_sum(src, seg, n):
    return jax.ops.segment_sum(src, seg, n)
kernel_name = 'mk_perceiver_d1_seqx_r8_60ffd0'

def setup_inputs(seed: int=0):
    np.random.seed(seed)
    _w = jnp.asarray

    def _rec_inputs():
        import jax
        import jax.numpy as jnp
        _rk = jax.random.key(seed)
        x = -0.0005207 + 1.001 * jax.random.normal(jax.random.fold_in(_rk, 1), (1, 128, 512), jnp.float32)
        _lenS = 128 - jax.random.randint(jax.random.fold_in(_rk, 7), (1,), 0, max(1, 128 // 4) + 1, jnp.int32)
        _lenS2 = 2048 - jax.random.randint(jax.random.fold_in(_rk, 8), (1,), 0, max(1, 2048 // 4) + 1, jnp.int32)
        _ctx_4096P = jax.random.normal(jax.random.fold_in(_rk, 11), (1, 16, 512), jnp.float32)
        _ctx_4096c = jax.random.dirichlet(jax.random.fold_in(_rk, 511), 0.3 * jnp.ones((16,), jnp.float32), (1, 2048))
        _ctx_4096t = jnp.einsum('bsk,bkd->bsd', _ctx_4096c, _ctx_4096P)
        _ctx_4096t = _ctx_4096t * jax.lax.rsqrt(jnp.mean(jnp.square(_ctx_4096t)) + 1e-12) * 0.953939
        ctx_4096 = -0.00010331 + 0.999899 * (_ctx_4096t + 0.3 * jax.random.normal(jax.random.fold_in(_rk, 611), (1, 2048, 512), jnp.float32))
        return (x, ctx_4096)
    x, ctx_4096 = _rec_inputs()

    def _L0_xattn_setup():
        import jax, jax.numpy as jnp
        import numpy as np
        B, Q, D = (8, 64, 512)
        CTX = 512
        H, KV, HD = (16, 4, 96)
        G = H // KV
        key = jax.random.key(seed)
        ks = jax.random.split(key, 6)
        s = 0.02
        return {'latents': jax.random.normal(ks[0], (B, Q, D), jnp.float32), 'context': jax.random.normal(ks[1], (B, CTX, D), jnp.float32), 'Wq': jax.random.normal(ks[2], (H * HD, D), jnp.float32) * s, 'Wk': jax.random.normal(ks[3], (KV * HD, D), jnp.float32) * s, 'Wv': jax.random.normal(ks[4], (KV * HD, D), jnp.float32) * s, 'Wo': jax.random.normal(ks[5], (D, H * HD), jnp.float32) * s}
    _L0_xattn_all = _L0_xattn_setup()
    _L0_xattn_in = {k: v for k, v in _L0_xattn_all.items() if k in ('Wq', 'Wk', 'Wv', 'Wo')}
    del _L0_xattn_all

    def _L0_attn_setup():
        import jax, jax.numpy as jnp
        import numpy as np
        H = 512
        D = 1024
        N = 16
        K = 4
        R = 32
        BATCH = 1
        L = 256
        EPS = 1e-06

        def _rmsnorm(x, w):
            return x * jax.lax.rsqrt(jnp.mean(x * x, axis=-1, keepdims=True) + EPS) * w
        key = jax.random.key(seed)
        ks = jax.random.split(key, 10)
        s = 0.02
        return {'hidden_states': jax.random.normal(ks[0], (BATCH, L, H), jnp.float32), 'W_in': jax.random.normal(ks[1], (2 * D, H), jnp.float32) * s, 'conv_w': jax.random.normal(ks[2], (D, K), jnp.float32) * s, 'conv_b': jax.random.normal(ks[3], (D,), jnp.float32) * s, 'Wx': jax.random.normal(ks[4], (R + 2 * N, D), jnp.float32) * s, 'dt_ln_w': jnp.ones((R,), jnp.float32), 'b_ln_w': jnp.ones((N,), jnp.float32), 'c_ln_w': jnp.ones((N,), jnp.float32), 'Wdt': jax.random.normal(ks[5], (D, R), jnp.float32) * s, 'dt_bias': jax.random.normal(ks[6], (D,), jnp.float32) * s, 'A': -jnp.exp(jax.random.normal(ks[7], (D, N), jnp.float32) * 0.5), 'D_param': jnp.ones((D,), jnp.float32), 'W_out': jax.random.normal(ks[8], (H, D), jnp.float32) * s}
    _L0_attn_all = _L0_attn_setup()
    _L0_attn_in = {k: v for k, v in _L0_attn_all.items() if k in ('W_in', 'conv_w', 'conv_b', 'Wx', 'dt_ln_w', 'b_ln_w', 'c_ln_w', 'Wdt', 'dt_bias', 'A', 'D_param', 'W_out')}
    del _L0_attn_all

    def _L0_ffn_setup():
        import jax, jax.numpy as jnp
        import numpy as np
        GROUP_SIZE = 128

        def dequantize(imatrix, scales, zeros, group_size, out_dtype):
            rs = jnp.repeat(scales, group_size, axis=0)
            rz = jnp.repeat(zeros, group_size, axis=0)
            return ((imatrix.astype(rs.dtype) - rz.astype(rs.dtype)) * rs).astype(out_dtype)
        key = jax.random.key(seed)
        ks = jax.random.split(key, 10)
        H, I, G = (512, 1792, GROUP_SIZE)
        B, S = (4, 256)
        x = jax.random.normal(ks[0], (B, S, H), dtype=jnp.float32)
        gate_w = jax.random.randint(ks[1], (H, I), 0, 16, dtype=jnp.int32)
        gate_z = jax.random.randint(ks[2], (H // G, I), 0, 16, dtype=jnp.int32)
        gate_s = jax.random.uniform(ks[3], (H // G, I), dtype=jnp.float32) * 0.01
        up_w = jax.random.randint(ks[4], (H, I), 0, 16, dtype=jnp.int32)
        up_z = jax.random.randint(ks[5], (H // G, I), 0, 16, dtype=jnp.int32)
        up_s = jax.random.uniform(ks[6], (H // G, I), dtype=jnp.float32) * 0.01
        down_w = jax.random.randint(ks[7], (I, H), 0, 16, dtype=jnp.int32)
        down_z = jax.random.randint(ks[8], (I // G, H), 0, 16, dtype=jnp.int32)
        down_s = jax.random.uniform(ks[9], (I // G, H), dtype=jnp.float32) * 0.01
        return {'x': x, 'gate_w': gate_w, 'gate_z': gate_z, 'gate_s': gate_s, 'up_w': up_w, 'up_z': up_z, 'up_s': up_s, 'down_w': down_w, 'down_z': down_z, 'down_s': down_s}
    _L0_ffn_all = _L0_ffn_setup()
    _L0_ffn_in = {k: v for k, v in _L0_ffn_all.items() if k in ('gate_w', 'gate_z', 'gate_s', 'up_w', 'up_z', 'up_s', 'down_w', 'down_z', 'down_s')}
    del _L0_ffn_all
    return {'x': x, 'ctx_4096': ctx_4096, 'L0_xattn_Wq': _L0_xattn_in['Wq'], 'L0_xattn_Wk': _L0_xattn_in['Wk'], 'L0_xattn_Wv': _L0_xattn_in['Wv'], 'L0_xattn_Wo': _L0_xattn_in['Wo'], 'L0_attn_W_in': _L0_attn_in['W_in'], 'L0_attn_conv_w': _L0_attn_in['conv_w'], 'L0_attn_conv_b': _L0_attn_in['conv_b'], 'L0_attn_Wx': _L0_attn_in['Wx'], 'L0_attn_dt_ln_w': _L0_attn_in['dt_ln_w'], 'L0_attn_b_ln_w': _L0_attn_in['b_ln_w'], 'L0_attn_c_ln_w': _L0_attn_in['c_ln_w'], 'L0_attn_Wdt': _L0_attn_in['Wdt'], 'L0_attn_dt_bias': _L0_attn_in['dt_bias'], 'L0_attn_A': _L0_attn_in['A'], 'L0_attn_D_param': _L0_attn_in['D_param'], 'L0_attn_W_out': _L0_attn_in['W_out'], 'L0_ffn_gate_w': _L0_ffn_in['gate_w'], 'L0_ffn_gate_z': _L0_ffn_in['gate_z'], 'L0_ffn_gate_s': _L0_ffn_in['gate_s'], 'L0_ffn_up_w': _L0_ffn_in['up_w'], 'L0_ffn_up_z': _L0_ffn_in['up_z'], 'L0_ffn_up_s': _L0_ffn_in['up_s'], 'L0_ffn_down_w': _L0_ffn_in['down_w'], 'L0_ffn_down_z': _L0_ffn_in['down_z'], 'L0_ffn_down_s': _L0_ffn_in['down_s']}

def reference(x, ctx_4096, L0_xattn_Wq, L0_xattn_Wk, L0_xattn_Wv, L0_xattn_Wo, L0_attn_W_in, L0_attn_conv_w, L0_attn_conv_b, L0_attn_Wx, L0_attn_dt_ln_w, L0_attn_b_ln_w, L0_attn_c_ln_w, L0_attn_Wdt, L0_attn_dt_bias, L0_attn_A, L0_attn_D_param, L0_attn_W_out, L0_ffn_gate_w, L0_ffn_gate_z, L0_ffn_gate_s, L0_ffn_up_w, L0_ffn_up_z, L0_ffn_up_s, L0_ffn_down_w, L0_ffn_down_z, L0_ffn_down_s):
    import jax
    import jax.numpy as jnp

    def _L0_xattn_ref(latents, context, Wq, Wk, Wv, Wo):
        import jax, jax.numpy as jnp
        import numpy as np
        B, Q, D = (8, 64, 512)
        CTX = 512
        H, KV, HD = (16, 4, 96)
        G = H // KV
        b, q_len, _ = latents.shape
        hidden = jnp.concatenate([context, latents], axis=1)
        s_len = hidden.shape[1]
        q = (latents @ Wq.T).reshape(b, q_len, H, HD)
        k = (hidden @ Wk.T).reshape(b, s_len, KV, HD)
        v = (hidden @ Wv.T).reshape(b, s_len, KV, HD)
        q = q.transpose(0, 2, 1, 3).reshape(b, KV, G, q_len, HD)
        k = k.transpose(0, 2, 1, 3)
        v = v.transpose(0, 2, 1, 3)
        scale = 1.0 / jnp.sqrt(jnp.asarray(HD, q.dtype))
        scores = jnp.einsum('bkgqd,bksd->bkgqs', q, k) * scale
        attn = jax.nn.softmax(scores.astype(jnp.float32), axis=-1).astype(q.dtype)
        out = jnp.einsum('bkgqs,bksd->bkgqd', attn, v)
        out = out.reshape(b, H, q_len, HD).transpose(0, 2, 1, 3).reshape(b, q_len, H * HD)
        return out @ Wo.T

    def _L0_attn_ref(hidden_states, W_in, conv_w, conv_b, Wx, dt_ln_w, b_ln_w, c_ln_w, Wdt, dt_bias, A, D_param, W_out):
        import jax, jax.numpy as jnp
        import numpy as np
        H = 512
        D = 1024
        N = 16
        K = 4
        R = 32
        BATCH = 1
        L = 256
        EPS = 1e-06

        def _rmsnorm(x, w):
            return x * jax.lax.rsqrt(jnp.mean(x * x, axis=-1, keepdims=True) + EPS) * w
        proj = hidden_states @ W_in.T
        u, gate = jnp.split(proj, 2, axis=-1)
        x = jnp.transpose(u, (0, 2, 1))
        x = jax.lax.conv_general_dilated(x, conv_w[:, None, :], window_strides=(1,), padding=[(K - 1, 0)], dimension_numbers=('NCH', 'OIH', 'NCH'), feature_group_count=D)
        u = jax.nn.silu(jnp.transpose(x, (0, 2, 1)) + conv_b)
        ssm_p = u @ Wx.T
        dt, Bm, Cm = jnp.split(ssm_p, [R, R + N], axis=-1)
        dt = _rmsnorm(dt, dt_ln_w)
        Bm = _rmsnorm(Bm, b_ln_w)
        Cm = _rmsnorm(Cm, c_ln_w)
        delta = jax.nn.softplus(dt @ Wdt.T + dt_bias)

        def step(state, xs):
            d_t, B_t, C_t, u_t = xs
            dA = jnp.exp(d_t[..., None] * A)
            state = dA * state + (d_t * u_t)[..., None] * B_t[:, None, :]
            y_t = jnp.einsum('bdn,bn->bd', state, C_t)
            return (state, y_t)
        init = jnp.zeros((hidden_states.shape[0], D, N), hidden_states.dtype)
        xs = (jnp.swapaxes(delta, 0, 1), jnp.swapaxes(Bm, 0, 1), jnp.swapaxes(Cm, 0, 1), jnp.swapaxes(u, 0, 1))
        _, ys = jax.lax.scan(step, init, xs)
        y = jnp.swapaxes(ys, 0, 1) + u * D_param
        y = y * jax.nn.silu(gate)
        return y @ W_out.T

    def _L0_ffn_ref(x, gate_w, gate_z, gate_s, up_w, up_z, up_s, down_w, down_z, down_s):
        import jax, jax.numpy as jnp
        import numpy as np
        GROUP_SIZE = 128

        def dequantize(imatrix, scales, zeros, group_size, out_dtype):
            rs = jnp.repeat(scales, group_size, axis=0)
            rz = jnp.repeat(zeros, group_size, axis=0)
            return ((imatrix.astype(rs.dtype) - rz.astype(rs.dtype)) * rs).astype(out_dtype)
        dt = x.dtype
        gate_proj = dequantize(gate_w, gate_s, gate_z, GROUP_SIZE, dt)
        up_proj = dequantize(up_w, up_s, up_z, GROUP_SIZE, dt)
        down_proj = dequantize(down_w, down_s, down_z, GROUP_SIZE, dt)
        gate = jax.nn.silu(jnp.dot(x, gate_proj))
        up = jnp.dot(x, up_proj)
        return jnp.dot(gate * up, down_proj)
    x = x + _L0_xattn_ref(_layernorm(x, axis=-1), ctx_4096, L0_xattn_Wq, L0_xattn_Wk, L0_xattn_Wv, L0_xattn_Wo)
    x = x + _L0_attn_ref(_layernorm(x, axis=-1), L0_attn_W_in, L0_attn_conv_w, L0_attn_conv_b, L0_attn_Wx, L0_attn_dt_ln_w, L0_attn_b_ln_w, L0_attn_c_ln_w, L0_attn_Wdt, L0_attn_dt_bias, L0_attn_A, L0_attn_D_param, L0_attn_W_out)
    x = x + _L0_ffn_ref(_layernorm(x, axis=-1), L0_ffn_gate_w, L0_ffn_gate_z, L0_ffn_gate_s, L0_ffn_up_w, L0_ffn_up_z, L0_ffn_up_s, L0_ffn_down_w, L0_ffn_down_z, L0_ffn_down_s)
    return x

_drawn_inputs = setup_inputs


def setup_inputs(seed=0):
    import zlib

    import numpy as np

    out = dict(_drawn_inputs(seed))
    spreads = {'L0_attn_dt_ln_w': (1.0, 0.6),
     'L0_attn_b_ln_w': (1.0, 0.6),
     'L0_attn_c_ln_w': (1.0, 0.6),
     'L0_attn_D_param': (1.0, 0.6)}
    factors = {'L0_xattn_Wq': 4.37,
     'L0_xattn_Wk': 4.307,
     'L0_attn_W_in': 5.036,
     'L0_attn_conv_w': 5.462,
     'L0_attn_conv_b': 5.472,
     'L0_attn_Wx': 5.896,
     'L0_attn_Wdt': 8.0,
     'L0_attn_dt_bias': 8.0,
     'L0_attn_A': 8.0,
     'L0_attn_W_out': 4.764}
    for name, (base, spread) in spreads.items():
        noise = np.random.default_rng([zlib.crc32(name.encode()), seed]).standard_normal(out[name].shape)
        drawn = base * np.exp(spread * noise) if base else spread * noise
        out[name] = jnp.asarray(drawn.astype(out[name].dtype))
    for name, factor in factors.items():
        out[name] = (out[name] * factor).astype(out[name].dtype)
    return out
```

```python
from contextlib import ExitStack

import concourse.bass as bass
from concourse import mybir

F32 = mybir.dt.float32
F32R = mybir.dt.float32r
I32 = mybir.dt.int32
ALU = mybir.AluOpType
ACT = mybir.ActivationFunctionType
AX_X = mybir.AxisListType.X

P = 128
T = 128
D = 512
KD = D // P
CTX = 2048
S = CTX + T
KV, G, HD = 4, 4, 96
HK = HD + 1
VW = HD + 2
CH = 256
NCH = 1 + CTX // CH
KT = S // P
NT = KV * KT
LAG = 3
DI = 1024
DT = DI // P
N = 16
R = 32
TAPS = 4
I = 1792
IT = I // P
GI = 4
ZU = 256
SCALE = float(HD) ** -0.5
LN_EPS = 1e-5
RMS_EPS = 1e-6


def chunk_cols(j):
    return (CTX, CTX + T) if j == 0 else ((j - 1) * CH, j * CH)


def build(nc, A, out):
    with ExitStack() as ctx:
        count = [0]

        def sem(name):
            return ctx.enter_context(nc.semaphore(name))

        def bank(name):
            return ctx.enter_context(nc.psum_tensor(name, [P, 512], F32))

        def at(offset, name, shape, dt=F32):
            with ExitStack() as hold:
                if offset:
                    count[0] += 1
                    hold.enter_context(nc.sbuf_tensor(f"skip{count[0]}", [P, offset // 4], F32))
                return hold.enter_context(nc.sbuf_tensor(name, shape, dt))

        class Row:
            def __init__(self, start):
                self.at = start

            def put(self, name, shape, dt=F32):
                n = 4
                for s in shape[1:]:
                    n *= s
                t = at(self.at, name, shape, dt)
                self.at += (n + 31) // 32 * 32
                return t

        fixed = Row(0)
        x_res = fixed.put("x_res", [P, D])
        x_n = fixed.put("x_n", [P, D])
        ident = fixed.put("ident", [P, P])
        conv_w = fixed.put("conv_w", [P, DT, TAPS])
        conv_b = fixed.put("conv_b", [P, DT])
        a_par = fixed.put("a_par", [P, DT, N])
        d_par = fixed.put("d_par", [P, DT])
        ln_w = fixed.put("ln_w", [R + 2 * N, 1])
        stats = fixed.put("stats", [P, 8])
        norm = fixed.put("norm", [P, 8])
        eps = fixed.put("eps", [P, 2])
        neg_max = fixed.put("neg_max", [P, HD + KV * G])
        part_max = fixed.put("part_max", [P, G, NCH])
        ones_row = fixed.put("ones_row", [P, HD])
        zs = fixed.at
        x_nT = at(zs, "x_nT", [P, KD, T])
        z_b = [at(zs + 1024 * i, f"z_b{i}", [P, ZU], I32) for i in range(2)]
        s_b = [at(zs + 2048 + 1024 * i, f"s_b{i}", [P, ZU]) for i in range(2)]
        k_at = zs + 4096

        keys = Row(k_at)
        KH = keys.put("KH", [HK, KV, S], F32R)
        kl_at = keys.at
        KL = keys.put("KL", [HK, KV, S], F32R)
        vh_at = keys.at
        VH = keys.put("VH", [P, KV, KT, VW], F32R)
        vl_at = keys.at
        VL = keys.put("VL", [P, KV, KT, VW], F32R)
        q_at = keys.at
        QH = keys.put("QH", [HK, KV, G * T], F32R)
        QL = keys.put("QL", [HK, KV, G * T], F32R)
        r_at = keys.at

        proj = Row(r_at)
        WKH, WKL, WVH, WVL = [proj.put(n, [P, KD, KV * HD], F32R) for n in ("WKH", "WKL", "WVH", "WVL")]
        HH = [proj.put(f"HH{i}", [P, KD, CH], F32R) for i in range(2)]
        HL = [proj.put(f"HL{i}", [P, KD, CH], F32R) for i in range(2)]
        c_raw = [proj.put(f"c_raw{i}", [P, KD, CH]) for i in range(2)]
        w_raw = [proj.put(f"w_raw{i}", [P, KD, KV * HD]) for i in range(2)]

        att = Row(r_at)
        PR = [att.put(f"PR{i}", [P, G * T]) for i in range(3)]
        PH = [att.put(f"PH{i}", [P, G * T], F32R) for i in range(4)]
        PL = [att.put(f"PL{i}", [P, G * T], F32R) for i in range(4)]
        WO = [att.put(f"WO{i}", [HD, G, D]) for i in range(2)]
        w_out = att.put("w_out", [P, DT, D])
        o_raw = att.put("o_raw", [HK, G * T])
        o_n = att.put("o_n", [HD, G * T])
        end_att = att.at

        w_gate = at(k_at, "w_gate", [P, KD, I])
        w_up = at(kl_at, "w_up", [P, KD, I])
        tail = KD * I * 4
        w_x = at(k_at + tail, "w_x", [P, DT, R + 2 * N])
        w_dt = at(k_at + tail + 2048, "w_dt", [R + 1, DI])
        w_dn = at(vh_at, "w_dn", [P, IT - 1, D])
        w_dnx = at(kl_at + tail, "w_dnx", [P, 1, D])
        w_inu = at(vl_at, "w_inu", [P, KD, DI])
        w_ing = at(q_at, "w_ing", [P, KD, DI])

        mam = Row(r_at)
        B_b = mam.put("B_b", [P, N, T])
        C_b = mam.put("C_b", [P, N, T])
        dA = [mam.put(f"dA{i}", [P, N, T]) for i in range(2)]
        u_c = mam.put("u_c", [P, DT, T])
        assert mam.at <= r_at + 22528 + 16384
        delta = at(end_att - 4096, "delta", [P, DT, T])
        u_raw = at(r_at + 2 * 8192, "u_raw", [P, DT, T])
        sig = at(r_at + 3 * 8192, "sig", [P, DT, T])
        dBu = [at(vl_at + 8192 * i, f"dBu{i}", [P, N, T]) for i in range(2)]
        du = at(vl_at + 16384, "du", [P, DT, T])
        g_s = at(vl_at + 20480, "g_s", [P, DT, T])
        g_raw = at(q_at, "g_raw", [P, DT, T])
        x_T = x_n[:, :].rearrange("p (k t) -> p k t", k=KD)
        small = Row(r_at + 22528 + 16384 - 2048)
        sp = small.put("sp", [P, R + 2 * N])
        sq = small.put("sq", [P, R + 2 * N])
        dt_t = small.put("dt_t", [R + 1, T])
        bc_t = small.put("bc_t", [R + 2 * N, T])
        assert small.at <= r_at + 22528 + 16384
        y2 = [at(q_at + 4096 + 512 * i, f"y2{i}", [P, T]) for i in range(2)]
        y1 = [at(q_at + 5120 + 512 * i, f"y1{i}", [P, T]) for i in range(2)]

        ffn = Row(r_at)
        f_sig = [ffn.put(f"f_sig{i}", [P, GI * T]) for i in range(2)]
        h_T = ffn.put("h_T", [P, IT, T])
        y_out = ffn.put("y_out", [P, D])

        banks = [bank(f"bank{i}") for i in range(8)]
        aux = [[banks[4], banks[5]], [banks[6], banks[7]]]

        names = (
            "x_in wk_in wv_in wo_in0 wo_in1 wout_in winu_in wing_in wx_in par_in ctx_in0 ctx_in1 wq_in0 wq_in1 "
            "z_in0 z_in1 wgate_in wup_in wdn_in out_done "
            "consts pads stat_ok rstd_ok xn_ok wk_split wv_split ctx_split wraw_free wq_free raw_free "
            "kv_filled kv_high kv_free aux_filled0 aux_filled1 aux_free0 aux_free1 q_high xT_copy xT_high tail_low "
            "proj_done q_ok max_ok negmax_ok s_filled exp_ok ph_ok pl_pool pl_dve pv_ok head_done o_raw_ok recip_ok on_ok "
            "o_proj x1_ok deq_sub deq_ok x2T_tr x2T_ok u_filled g_filled uraw_ok conv_a conv_ok sil_a u_ok graw_ok gsil_a gs_ok "
            "ssm_filled sp_ok ss_ok rms_ok spn_ok tr_filled dtbc_ok delta_filled dl_a delta_ok du_ok "
            "bb_filled bb_ok zero_ok dA_ok dBu_ok scan_ok yc_ok y_filled y1_ok y2_ok y2_used mo_filled x2_ok x3T_tr x3T_ok "
            "gu_filled fs_a h_part h_ok gu_free down_filled fin_ok act_seq dve_seq"
        ).split()
        q = {n: sem(n) for n in names}
        aux_filled = [q["aux_filled0"], q["aux_filled1"]]
        aux_free = [q["aux_free0"], q["aux_free1"]]

        aux_items = []
        step_extra = {}

        def add_aux(item):
            aux_items.append(item)

        pre = {}
        pre[0] = [("q", 0)]
        for j in range(1, NCH):
            pre[j] = [("mx", 0, j - 1)]
            if j in (1, 3, 5):
                pre[j].append(("q", (j + 1) // 2))
        pre[NCH - 1] += [("mx", 0, NCH - 1), ("nm", 0)]
        for step in range(NT + LAG + 8):
            todo = []
            h, t = step // KT, step % KT
            if h + 1 < KV:
                todo += [("mx", h + 1, j) for j in range(NCH) if t == 3 * j // 2]
                if t == 15:
                    todo.append(("nm", h + 1))
            if h >= 1 and t == LAG + 3:
                todo.append(("bc", h - 1))
            step_extra[step] = todo
        add_aux(("xT",))
        for j in range(NCH):
            for it in pre[j]:
                add_aux(it)
        for step in range(NT + LAG + 8):
            for it in step_extra[step]:
                add_aux(it)
        aux_index = {it: i for i, it in enumerate(aux_items)}

        def aux_of(item):
            i = aux_index[item]
            return i % 2, i // 2

        def piece(kind, g, c):
            cols = slice(c * ZU, (c + 1) * ZU)
            if kind == "down":
                return w_dn[:, g, cols] if g < IT - 1 else w_dnx[:, 0, cols]
            return (w_gate if kind == "gate" else w_up)[:, g, cols]

        def deq_at(s):
            h, t = s // KT, s % KT
            if h == 0 or s >= NT:
                return 0
            n = len(units_of(h - 1))
            return n * (t + 1) // KT - n * t // KT

        def low_part(s):
            if s % 3 == 2:
                return q["pl_dve"], s // 3 + 1
            return q["pl_pool"], s - s // 3 + 1

        block = ctx.enter_context(nc.Block())

        @block.sync
        def _(sp_q):
            def load(dst, src, s):
                sp_q.dma_start(dst, src).then_inc(q[s], 16)

            load(x_res[:], A["x"], "x_in")
            load(w_raw[0][:], A["wk"], "wk_in")
            load(c_raw[0][:], A["ctx"][:, :, 0:CH], "ctx_in0")
            load(w_raw[1][:], A["wv"], "wv_in")
            load(c_raw[1][:], A["ctx"][:, :, CH:2 * CH], "ctx_in1")
            nq = 0
            for j in range(1, NCH):
                if nq < KV:
                    if nq < 2:
                        sp_q.wait_ge(q["wraw_free"], nq + 1)
                    else:
                        sp_q.wait_ge(q["wq_free"], nq - 1)
                    load(w_raw[nq % 2][:], A["wq"][:, :, nq * G * HD:(nq + 1) * G * HD], f"wq_in{nq % 2}")
                    nq += 1
                if j + 2 < NCH:
                    sp_q.wait_ge(q["raw_free"], j)
                    load(c_raw[(j + 1) % 2][:], A["ctx"][:, :, (j + 1) * CH:(j + 2) * CH], f"ctx_in{(j + 1) % 2}")
            load(conv_w[:], A["conv_w"], "par_in")
            load(conv_b[:], A["conv_b"], "par_in")
            load(a_par[:], A["a"], "par_in")
            load(d_par[:], A["d"], "par_in")
            load(ln_w[0:R, :], A["ln_dt"], "par_in")
            load(ln_w[R:R + N, :], A["ln_b"], "par_in")
            load(ln_w[R + N:R + 2 * N, :], A["ln_c"], "par_in")
            sp_q.wait_ge(q["proj_done"], 1)
            load(WO[0][:], A["wo"][:, 0:G, :], "wo_in0")
            load(WO[1][:], A["wo"][:, G:2 * G, :], "wo_in1")
            load(w_out[:], A["w_out"], "wout_in")
            unit = 0
            for h in range(KV):
                sp_q.wait_ge(q["head_done"], h + 1)
                if h == KV - 1:
                    load(w_ing[:], A["w_in"][:, :, DI:2 * DI], "wing_in")
                    load(w_x[:], A["w_x"], "wx_in")
                    load(w_dt[0:R, :], A["w_dt"], "wx_in")
                    load(w_dt[R:R + 1, :], A["dt_bias"], "wx_in")
                load(w_gate[:, h, :].bitcast(I32), A["gate_w"][:, h, :], "wgate_in")
                load(w_up[:, h, :].bitcast(I32), A["up_w"][:, h, :], "wup_in")
                lo, hi = down_tiles(h)
                load(w_dn[:, lo:min(hi, IT - 1), :].bitcast(I32), A["down_w"][:, lo:min(hi, IT - 1), :], "wdn_in")
                if hi == IT:
                    load(w_dnx[:].bitcast(I32), A["down_w"][:, IT - 1:IT, :], "wdn_in")
                if h == KV - 2:
                    load(w_inu[:], A["w_in"][:, :, 0:DI], "winu_in")
                for kind, g, c in units_of(h):
                    if unit >= 2:
                        sp_q.wait_ge(q["deq_ok"], unit - 1)
                    z, s = A[kind + "_z"], A[kind + "_s"]
                    cols = slice(c * ZU, (c + 1) * ZU)
                    load(z_b[unit % 2][:], z[g:g + 1, cols].to_broadcast([P, ZU]), f"z_in{unit % 2}")
                    load(s_b[unit % 2][:], s[g:g + 1, cols].to_broadcast([P, ZU]), f"z_in{unit % 2}")
                    unit += 1
                if h + 2 < KV:
                    sp_q.wait_ge(q["o_proj"], h + 1)
                    load(WO[h % 2][:], A["wo"][:, (h + 2) * G:(h + 3) * G, :], f"wo_in{h % 2}")
            sp_q.wait_ge(q["fin_ok"], 1)
            sp_q.dma_start(out, y_out[:]).then_inc(q["out_done"], 16)
            sp_q.wait_ge(q["out_done"], 16)

        @block.gpsimd
        def _(pool):
            pool.memset(ident[:], 0.0).then_inc(q["zero_ok"], 1)
            pool.memset(eps[:, 0:1], LN_EPS)
            pool.memset(eps[:, 1:2], RMS_EPS)
            pool.memset(neg_max[:], 0.0)
            pool.memset(ones_row[:], 1.0)
            pool.wait_ge(q["zero_ok"], 1)
            pool.affine_select(out=ident[:], in_=ident[:], compare_op=ALU.not_equal, fill=1.0, base=0,
                               pattern=[[-1, P]], channel_multiplier=1).then_inc(q["consts"], 1)
            for j in range(1, NCH):
                b = (j - 1) % 2
                pool.wait_ge(q[f"ctx_in{b}"], 16 * ((j - 1) // 2 + 1))
                if j >= 2:
                    pool.wait_ge(q["kv_filled"], kv_items_upto(j - 2))
                pool.tensor_scalar(HH[j % 2][:], c_raw[b][:], 1.0, None, ALU.mult).then_inc(q["ctx_split"], 1)
                pool.wait_ge(q["ctx_split"], 2 * j - 1)
                pool.tensor_tensor(HL[j % 2][:], c_raw[b][:], HH[j % 2][:].bitcast(F32),
                                   ALU.subtract).then_inc(q["ctx_split"], 1)
                pool.wait_ge(q["ctx_split"], 2 * j)
                pool.sem_inc(q["raw_free"], 1)
                if j == 1:
                    for m, (cells, value) in enumerate(((KH[HD:HK, :, :], 1.0), (KL[HD:HK, :, :], 0.0),
                                                        (QL[HD:HK, :, :], 0.0), (VH[:, :, :, HD:VW], 1.0),
                                                        (VL[:, :, :, HD:VW], 0.0))):
                        pool.memset(cells.bitcast(F32), value).then_inc(q["pads"], 1)
                        pool.wait_ge(q["pads"], m + 1)
            unit = 0
            todo = [u for h in range(KV) for u in units_of(h)]

            def scale_unit():
                nonlocal unit
                if unit >= len(todo):
                    return
                kind, g, c = todo[unit]
                pool.wait_ge(q["deq_sub"], unit + 1)
                w = piece(kind, g, c)
                pool.tensor_tensor(w, w, s_b[unit % 2][:], ALU.mult).then_inc(q["deq_ok"], 1)
                unit += 1

            for s in range(NT):
                if s % 3 != 2:
                    pool.wait_ge(q["ph_ok"], s + 1)
                    if s >= 4:
                        pool.wait_ge(q["pv_ok"], s - 3)
                    pool.tensor_tensor(PL[s % 4][:], PR[s % 3][:], PH[s % 4][:].bitcast(F32),
                                       ALU.subtract).then_inc(q["pl_pool"], 1)
                for _ in range(deq_at(s)):
                    scale_unit()
            for _ in range(len(units_of(KV - 1)) // 2):
                scale_unit()
            pool.wait_ge(q["delta_ok"], 2)
            for b in range(2):
                last = pool.memset(dA[b][:, :, 0:1], 0.0)
            last.then_inc(q["zero_ok"], 1)
            pool.wait_ge(q["bb_ok"], 4)
            for i in range(DT):
                pool.wait_ge(q["du_ok"], 1)
                if i >= 2:
                    pool.wait_ge(q["y_filled"], i - 1)
                pool.tensor_tensor(dBu[i % 2][:], B_b[:], du[:, i:i + 1, :].to_broadcast([P, N, T]),
                                   ALU.mult).then_inc(q["dBu_ok"], 1)
                scale_unit()
                scale_unit()
            assert unit == len(todo)

        @block.scalar
        def _(act):
            def rstd(src, dst, e, scale=1.0):
                act.activation(dst, src, ACT.Ln, bias=e, scale=scale).then_inc(q["act_seq"], 1)
                seq[0] += 1
                act.wait_ge(q["act_seq"], seq[0])
                return act.activation(dst, dst, ACT.Exp, scale=-0.5)

            seq = [0]

            def chain(ins):
                ins.then_inc(q["act_seq"], 1)
                seq[0] += 1
                act.wait_ge(q["act_seq"], seq[0])

            act.wait_ge(q["consts"], 1)
            act.wait_ge(q["stat_ok"], 1)
            rstd(stats[:, 7:8], norm[:, 0:1], eps[:, 0:1]).then_inc(q["rstd_ok"], 1)

            def evac_aux(item):
                pair, k = aux_of(item)
                act.wait_ge(aux_filled[pair], k + 1)
                src = aux[pair][0]
                if item[0] == "xT":
                    v = src[:, :].rearrange("p (k t) -> p k t", k=KD)
                    act.activation(x_nT[:], v, ACT.Copy).then_inc(q["xT_copy"], 1)
                    act.activation(HH[0][:, :, 0:T], v, ACT.Copy).then_inc(q["xT_high"], 1)
                elif item[0] == "q":
                    act.activation(QH[0:HD, item[1], :], src[0:HD, :], ACT.Copy).then_inc(q["q_high"], 1)
                elif item[0] == "nm":
                    act.activation(QH[HD:HK, item[1], :], src[HD:HK, :], ACT.Copy).then_inc(aux_free[pair], 1)

            evac_aux(("xT",))
            n = 0
            for j in range(NCH):
                lo, hi = chunk_cols(j)
                for part in range(kv_parts(j)):
                    act.wait_ge(q["kv_filled"], n + 1)
                    src = banks[n % 4]
                    if part < 2:
                        v = src[0:HD, 0:2 * (hi - lo)].rearrange("p (h t) -> p h t", h=2)
                        act.activation(KH[0:HD, 2 * part:2 * part + 2, lo:hi], v, ACT.Copy).then_inc(q["kv_high"], 1)
                    else:
                        v = src[:, 0:KV * HD].rearrange("p (h d) -> p h d", h=KV)
                        act.activation(VH[:, :, lo // P + part - 2, 0:HD], v, ACT.Copy).then_inc(q["kv_high"], 1)
                    n += 1
                for item in pre[j]:
                    if item[0] in ("q", "nm"):
                        evac_aux(item)

            for s in range(NT + LAG + 8):
                h, t = s // KT, s % KT
                if s < NT:
                    act.wait_ge(q["s_filled"], s + 1)
                    if s >= 3:
                        act.wait_ge(*low_part(s - 3))
                    elif s == 0:
                        act.wait_ge(q["proj_done"], 1)
                    act.activation(PR[s % 3][:], banks[s % 2][:, :], ACT.Exp, scale=SCALE).then_inc(q["exp_ok"], 1)
                    act.wait_ge(q["exp_ok"], s + 1)
                    if s >= 4:
                        act.wait_ge(q["pv_ok"], s - 3)
                    act.activation(PH[s % 4][:], PR[s % 3][:], ACT.Copy).then_inc(q["ph_ok"], 1)
                if s >= LAG and (s - LAG) % KT == KT - 1 and s - LAG < NT:
                    hd = (s - LAG) // KT
                    act.wait_ge(q["head_done"], hd + 1)
                    if hd >= 1:
                        act.wait_ge(q["on_ok"], hd)
                    act.activation(o_raw[:], banks[2][0:HK, :], ACT.Copy).then_inc(q["o_raw_ok"], 1)
                for item in step_extra[s]:
                    if item[0] == "nm":
                        evac_aux(item)

            act.wait_ge(q["stat_ok"], 2)
            rstd(stats[:, 7:8], norm[:, 0:1], eps[:, 0:1]).then_inc(q["rstd_ok"], 1)
            act.wait_ge(q["x2T_tr"], 1)
            act.activation(x_T, banks[4][:, :].rearrange("p (k t) -> p k t", k=KD), ACT.Copy).then_inc(q["x2T_ok"], 1)

            def sigmoid(dst, src):
                chain(act.activation(dst, src, ACT.Exp, scale=-1.0))
                chain(act.activation(dst, dst, ACT.Ln, bias=1.0))
                return act.activation(dst, dst, ACT.Exp, scale=-1.0)

            act.wait_ge(q["par_in"], 16 * 7)
            for half in range(2):
                tiles = range(4 * half, 4 * half + 4)
                act.wait_ge(q["u_filled"], half + 1)
                chain(act.activation(u_raw[:, 4 * half:4 * half + 4, :],
                                     banks[half][:, :].rearrange("p (i t) -> p i t", i=4), ACT.Copy))
                for i in tiles:
                    last = act.activation(u_c[:, i, :], u_raw[:, i, :], ACT.Identity,
                                          bias=conv_b[:, i:i + 1], scale=conv_w[:, i, TAPS - 1:TAPS])
                last.then_inc(q["conv_a"], 1)
            for half in range(2):
                sl = slice(4 * half, 4 * half + 4)
                act.wait_ge(q["conv_ok"], 4 * (half + 1))
                sigmoid(sig[:, sl, :], u_c[:, sl, :]).then_inc(q["sil_a"], 1)
            act.wait_ge(q["ssm_filled"], 1)
            act.activation(sp[:], banks[4][:, 0:R + 2 * N], ACT.Copy).then_inc(q["sp_ok"], 1)
            act.wait_ge(q["ss_ok"], 1)
            chain(act.activation(norm[:, 2:3], norm[:, 2:3], ACT.Ln, bias=eps[:, 1:2], scale=1.0 / R))
            chain(act.activation(norm[:, 3:5], norm[:, 3:5], ACT.Ln, bias=eps[:, 1:2], scale=1.0 / N))
            act.activation(norm[:, 2:5], norm[:, 2:5], ACT.Exp, scale=-0.5).then_inc(q["rms_ok"], 1)
            act.wait_ge(q["tr_filled"], 1)
            act.activation(dt_t[0:R, :], banks[5][0:R, 0:T], ACT.Copy, scale=ln_w[0:R, :]).then_inc(q["dtbc_ok"], 1)
            act.activation(bc_t[R:R + 2 * N, :], banks[5][R:R + 2 * N, 0:T], ACT.Copy,
                           scale=ln_w[R:R + 2 * N, :]).then_inc(q["dtbc_ok"], 1)
            for half in range(2):
                sl = slice(4 * half, 4 * half + 4)
                act.wait_ge(q["delta_filled"], half + 1)
                z = banks[6 + half][:, :].rearrange("p (i t) -> p i t", i=4)
                chain(act.activation(sig[:, sl, :], z, ACT.Abs))
                chain(act.activation(sig[:, sl, :], sig[:, sl, :], ACT.Exp, scale=-1.0))
                act.activation(sig[:, sl, :], sig[:, sl, :], ACT.Ln, bias=1.0).then_inc(q["dl_a"], 1)
            for k in range(8):
                act.wait_ge(q["bb_filled"], k + 1)
                dst = (B_b if k < 4 else C_b)[:, 4 * (k % 4):4 * (k % 4) + 4, :]
                src = banks[(0, 1, 4, 5)[k % 4]][:, :].rearrange("p (i t) -> p i t", i=4)
                act.activation(dst, src, ACT.Copy).then_inc(q["bb_ok"], 1)
            act.wait_ge(q["delta_ok"], 2)
            act.wait_ge(q["zero_ok"], 2)
            for i in range(DT):
                if i >= 2:
                    act.wait_ge(q["scan_ok"], i - 1)
                for m in range(N):
                    last = act.activation(dA[i % 2][:, m, 1:T], delta[:, i, 1:T], ACT.Exp, scale=a_par[:, i, m:m + 1])
                last.then_inc(q["dA_ok"], 1)
                if i == 0:
                    act.wait_ge(q["g_filled"], 2)
                    for half in range(2):
                        act.activation(g_raw[:, 4 * half:4 * half + 4, :],
                                       banks[2 + half][:, :].rearrange("p (i t) -> p i t", i=4),
                                       ACT.Copy).then_inc(q["graw_ok"], 1)
                    act.wait_ge(q["graw_ok"], 2)
                    sigmoid(g_s[:], g_raw[:]).then_inc(q["gsil_a"], 1)
            act.wait_ge(q["stat_ok"], 3)
            rstd(stats[:, 7:8], norm[:, 0:1], eps[:, 0:1]).then_inc(q["rstd_ok"], 1)
            act.wait_ge(q["x3T_tr"], 1)
            act.activation(x_T, banks[4][:, :].rearrange("p (k t) -> p k t", k=KD), ACT.Copy).then_inc(q["x3T_ok"], 1)
            for m in range(ffn_groups()):
                n = min(GI, IT - GI * m) * T
                act.wait_ge(q["gu_filled"], m + 1)
                if m >= 2:
                    act.wait_ge(q["h_part"], m - 1)
                sigmoid(f_sig[m % 2][:, 0:n], banks[2 * (m % 2)][:, 0:n]).then_inc(q["fs_a"], 1)

        @block.vector
        def _(dve):
            seq = [0]

            def chain(ins):
                ins.then_inc(q["dve_seq"], 1)
                seq[0] += 1
                dve.wait_ge(q["dve_seq"], seq[0])

            def norm_rows(k):
                chain(dve.bn_stats(stats[:, 0:6], x_res[:]))
                dve.bn_aggr(stats[:, 6:8], stats[:, 0:6]).then_inc(q["stat_ok"], 1)
                dve.wait_ge(q["stat_ok"], k + 1)
                dve.wait_ge(q["rstd_ok"], k + 1)
                dve.tensor_scalar(x_n[:], x_res[:], stats[:, 6:7], norm[:, 0:1],
                                  ALU.subtract, ALU.mult).then_inc(q["xn_ok"], 1)

            dve.wait_ge(q["x_in"], 16)
            norm_rows(0)
            dve.wait_ge(q["wk_in"], 16)
            chain(dve.tensor_copy(WKH[:], w_raw[0][:]))
            dve.tensor_tensor(WKL[:], w_raw[0][:], WKH[:].bitcast(F32), ALU.subtract).then_inc(q["wk_split"], 1)
            pair, k = aux_of(("xT",))
            dve.wait_ge(q["xT_high"], 1)
            dve.tensor_tensor(HL[0][:, :, 0:T], aux[pair][0][:, :].rearrange("p (k t) -> p k t", k=KD),
                              HH[0][:, :, 0:T].bitcast(F32), ALU.subtract).then_inc(q["tail_low"], 1)
            dve.wait_ge(q["tail_low"], 1)
            dve.sem_inc(aux_free[pair], 1)
            dve.wait_ge(q["wk_split"], 1)
            dve.sem_inc(q["wraw_free"], 1)
            dve.wait_ge(q["wv_in"], 16)
            chain(dve.tensor_copy(WVH[:], w_raw[1][:]))
            chain(dve.tensor_tensor(WVL[:], w_raw[1][:], WVH[:].bitcast(F32), ALU.subtract))
            dve.sem_inc(q["wv_split"], 1)
            dve.sem_inc(q["wraw_free"], 1)

            def take_aux(item):
                pair, k = aux_of(item)
                a, b = aux[pair]
                dve.wait_ge(aux_filled[pair], k + 1)
                if item[0] == "q":
                    h = item[1]
                    dve.wait_ge(q["q_high"], h + 1)
                    dve.tensor_tensor(QL[0:HD, h, :], a[0:HD, :], QH[0:HD, h, :].bitcast(F32),
                                      ALU.subtract).then_inc(aux_free[pair], 1)
                elif item[0] == "mx":
                    _, h, j = item
                    lo, hi = chunk_cols(j)
                    w = hi - lo
                    for m, bk in enumerate((a, b)):
                        last = dve.tensor_reduce(part_max[:, 2 * m:2 * m + 2, j],
                                                 bk[:, 0:2 * w].rearrange("p (g t) -> p g t", g=2), AX_X, ALU.max)
                    last.then_inc(aux_free[pair], 1)
                    if j == NCH - 1:
                        dve.wait_ge(aux_free[pair], k + 1)
                        dve.tensor_reduce(neg_max[:, HD + G * h:HD + G * (h + 1)], part_max[:], AX_X, ALU.max,
                                          negate=True).then_inc(q["max_ok"], 1)
                        dve.wait_ge(q["max_ok"], h + 1)

            def bc_take(hd):
                pair, k = aux_of(("bc", hd))
                dve.wait_ge(aux_filled[pair], k + 1)
                if hd >= 1:
                    dve.wait_ge(q["o_proj"], hd)
                dve.tensor_tensor(o_n[:], o_raw[0:HD, :], aux[pair][0][0:HD, :], ALU.mult).then_inc(q["on_ok"], 1)
                dve.wait_ge(q["on_ok"], hd + 1)
                dve.sem_inc(aux_free[pair], 1)

            unit = 0
            todo = [u for h in range(KV) for u in units_of(h)]
            owner = [h for h in range(KV) for _ in units_of(h)]

            def zero_unit():
                nonlocal unit
                if unit >= len(todo):
                    return
                kind, g, c = todo[unit]
                h = owner[unit]
                loads = h + 1 if (kind, g) != ("down", IT - 1) else KV + 1
                dve.wait_ge(q[{"gate": "wgate_in", "up": "wup_in", "down": "wdn_in"}[kind]], 16 * loads)
                dve.wait_ge(q[f"z_in{unit % 2}"], 32 * (unit // 2 + 1))
                w = piece(kind, g, c)
                dve.tensor_tensor(w, w.bitcast(I32), z_b[unit % 2][:], ALU.subtract).then_inc(q["deq_sub"], 1)
                unit += 1

            n = 0
            for j in range(NCH):
                lo, hi = chunk_cols(j)
                for part in range(kv_parts(j)):
                    dve.wait_ge(q["kv_high"], n + 1)
                    src = banks[n % 4]
                    if part < 2:
                        v = src[0:HD, 0:2 * (hi - lo)].rearrange("p (h t) -> p h t", h=2)
                        sl = slice(2 * part, 2 * part + 2)
                        dve.tensor_tensor(KL[0:HD, sl, lo:hi], v, KH[0:HD, sl, lo:hi].bitcast(F32),
                                          ALU.subtract).then_inc(q["kv_free"], 1)
                    else:
                        v = src[:, 0:KV * HD].rearrange("p (h d) -> p h d", h=KV)
                        kt = lo // P + part - 2
                        dve.tensor_tensor(VL[:, :, kt, 0:HD], v, VH[:, :, kt, 0:HD].bitcast(F32),
                                          ALU.subtract).then_inc(q["kv_free"], 1)
                    n += 1
                for item in pre[j]:
                    take_aux(item)

            dve.wait_ge(q["proj_done"], 1)
            for s in range(NT + LAG + 8):
                h, t = s // KT, s % KT
                if s < NT and s % 3 == 2:
                    dve.wait_ge(q["ph_ok"], s + 1)
                    if s >= 4:
                        dve.wait_ge(q["pv_ok"], s - 3)
                    dve.tensor_tensor(PL[s % 4][:], PR[s % 3][:], PH[s % 4][:].bitcast(F32),
                                      ALU.subtract).then_inc(q["pl_dve"], 1)
                for _ in range(deq_at(s)):
                    zero_unit()
                for item in step_extra[s]:
                    if item[0] == "mx":
                        take_aux(item)
                fin = s - LAG - KT
                if fin >= 0 and fin % KT in (0, 1):
                    hd = fin // KT
                    if fin % KT == 0:
                        dve.wait_ge(q["o_raw_ok"], hd + 1)
                    for m in range(2):
                        cols = slice((2 * (fin % KT) + m) * T, (2 * (fin % KT) + m + 1) * T)
                        dve.reciprocal(o_raw[HD:HK, cols], o_raw[HD:HK, cols]).then_inc(q["recip_ok"], 1)
                if fin >= 0 and fin % KT == 4:
                    hd = fin // KT
                    bc_take(hd)
            dve.wait_ge(q["o_proj"], KV)
            chain(dve.tensor_tensor(x_res[:], banks[3][:, :], x_res[:], ALU.add))
            norm_rows(1)
            for half in range(2):
                dve.wait_ge(q["conv_a"], half + 1)
                for shift in range(1, TAPS):
                    for i in range(4 * half, 4 * half + 4):
                        dve.scalar_tensor_tensor(u_c[:, i, shift:T], u_raw[:, i, 0:T - shift],
                                                 conv_w[:, i, TAPS - 1 - shift:TAPS - shift], u_c[:, i, shift:T],
                                                 ALU.mult, ALU.add).then_inc(q["conv_ok" if shift == TAPS - 1 else "dve_seq"], 1)
                        if shift < TAPS - 1:
                            seq[0] += 1
                    if shift < TAPS - 1:
                        dve.wait_ge(q["dve_seq"], seq[0])
            for half in range(2):
                sl = slice(4 * half, 4 * half + 4)
                dve.wait_ge(q["sil_a"], half + 1)
                dve.tensor_tensor(u_c[:, sl, :], u_c[:, sl, :], sig[:, sl, :], ALU.mult).then_inc(q["u_ok"], 1)
            for _ in range(len(units_of(KV - 1)) // 2):
                zero_unit()
            dve.memset(dt_t[R:R + 1, :], 1.0).then_inc(q["dtbc_ok"], 1)
            dve.wait_ge(q["sp_ok"], 1)
            chain(dve.tensor_tensor(sq[:], sp[:], sp[:], ALU.mult))
            dve.tensor_reduce(norm[:, 2:3], sq[:, 0:R], AX_X, ALU.add)
            dve.tensor_reduce(norm[:, 3:5], sq[:, R:R + 2 * N].rearrange("p (a n) -> p a n", a=2), AX_X,
                              ALU.add).then_inc(q["ss_ok"], 1)
            dve.wait_ge(q["rms_ok"], 1)
            for a, (lo, hi) in enumerate(((0, R), (R, R + N), (R + N, R + 2 * N))):
                dve.tensor_scalar(sp[:, lo:hi], sp[:, lo:hi], norm[:, 2 + a:3 + a], None,
                                  ALU.mult).then_inc(q["spn_ok"], 1)
            for half in range(2):
                sl = slice(4 * half, 4 * half + 4)
                dve.wait_ge(q["dl_a"], half + 1)
                z = banks[6 + half][:, :].rearrange("p (i t) -> p i t", i=4)
                dve.scalar_tensor_tensor(delta[:, sl, :], z, 0.0, sig[:, sl, :], ALU.max, ALU.add).then_inc(q["delta_ok"], 1)
            dve.wait_ge(q["delta_ok"], 2)
            dve.tensor_tensor(du[:], delta[:], u_c[:], ALU.mult).then_inc(q["du_ok"], 1)

            def gate_out(i):
                dve.wait_ge(q["y_filled"], i + 1)
                if i >= 2:
                    dve.wait_ge(q["y2_used"], i - 1)
                dve.scalar_tensor_tensor(y1[i % 2][:], u_c[:, i, :], d_par[:, i:i + 1], banks[6 + i % 2][:, 0:T],
                                         ALU.mult, ALU.add).then_inc(q["y1_ok"], 1)
                dve.wait_ge(q["y1_ok"], i + 1)
                dve.tensor_tensor(y2[i % 2][:], y1[i % 2][:], g_s[:, i, :], ALU.mult).then_inc(q["y2_ok"], 1)

            for i in range(DT):
                b = i % 2
                dve.wait_ge(q["dA_ok"], i + 1)
                dve.wait_ge(q["dBu_ok"], i + 1)
                flat = dBu[b][:].rearrange("p n t -> p (n t)")
                dve.tensor_tensor_scan(flat, dA[b][:].rearrange("p n t -> p (n t)"), flat, 0.0,
                                       ALU.mult, ALU.add).then_inc(q["scan_ok"], 1)
                dve.wait_ge(q["scan_ok"], i + 1)
                if i == 0:
                    dve.wait_ge(q["bb_ok"], 8)
                dve.tensor_tensor(dBu[b][:], dBu[b][:], C_b[:], ALU.mult).then_inc(q["yc_ok"], 1)
                if i == 0:
                    dve.wait_ge(q["gsil_a"], 1)
                    dve.tensor_tensor(g_s[:], g_s[:], g_raw[:], ALU.mult).then_inc(q["gs_ok"], 1)
                    dve.wait_ge(q["gs_ok"], 1)
                else:
                    gate_out(i - 1)
                zero_unit()
                zero_unit()
            gate_out(DT - 1)
            dve.wait_ge(q["mo_filled"], 1)
            chain(dve.tensor_tensor(x_res[:], banks[2][:, :], x_res[:], ALU.add))
            norm_rows(2)
            for m in range(ffn_groups()):
                n = min(GI, IT - GI * m) * T
                dve.wait_ge(q["fs_a"], m + 1)
                hs = h_T[:, GI * m:GI * m + n // T, :].rearrange("p i t -> p (i t)")
                chain(dve.tensor_tensor(f_sig[m % 2][:, 0:n], banks[2 * (m % 2)][:, 0:n], f_sig[m % 2][:, 0:n], ALU.mult))
                dve.tensor_tensor(hs, banks[2 * (m % 2) + 1][:, 0:n], f_sig[m % 2][:, 0:n],
                                  ALU.mult).then_inc(q["h_part"], 1)
            dve.wait_ge(q["down_filled"], 1)
            dve.tensor_tensor(y_out[:], banks[5][:, :], x_res[:], ALU.add).then_inc(q["fin_ok"], 1)

        @block.tensor
        def _(pe):
            def mm3(dst, wh, wl, xh, xl, start, stop):
                pe.matmul(dst, wh, xh, start=start, stop=False)
                pe.matmul(dst, wh, xl, start=False, stop=False)
                return pe.matmul(dst, wl, xh, start=False, stop=stop)

            def start_aux(item):
                pair, k = aux_of(item)
                if k >= 1:
                    pe.wait_ge(aux_free[pair], k)
                a, b = aux[pair]
                if item[0] == "xT":
                    pe.wait_ge(q["xn_ok"], 1)
                    pe.wait_ge(q["consts"], 1)
                    for k4 in range(KD):
                        last = pe.transpose(a[:, k4 * T:(k4 + 1) * T], x_n[:, k4 * P:(k4 + 1) * P], ident[:])
                elif item[0] == "q":
                    h = item[1]
                    pe.wait_ge(q["xT_copy"], 1)
                    pe.wait_ge(q[f"wq_in{h % 2}"], 16 * (h // 2 + 1))
                    for g in range(G):
                        for k4 in range(KD):
                            last = pe.matmul(a[0:HD, g * T:(g + 1) * T], w_raw[h % 2][:, k4, g * HD:(g + 1) * HD],
                                             x_nT[:, k4, :], start=(k4 == 0), stop=(k4 == KD - 1))
                elif item[0] == "mx":
                    _, h, j = item
                    lo, hi = chunk_cols(j)
                    if h == 0:
                        pe.wait_ge(q["kv_high"], kv_items_upto(j - 1) + 1)
                    pe.wait_ge(q["q_high"], h + 1)
                    for g in range(G):
                        bk = (a, b)[g // 2]
                        w = hi - lo
                        last = pe.matmul(bk[:, (g % 2) * w:(g % 2 + 1) * w], QH[0:HD, h, g * T:(g + 1) * T],
                                         KH[0:HD, h, lo:hi], start=True, stop=True)
                elif item[0] == "nm":
                    h = item[1]
                    pe.wait_ge(q["max_ok"], h + 1)
                    for g in range(G):
                        c = G * h + g
                        last = pe.matmul(a[0:HK, g * T:(g + 1) * T], neg_max[:, c:c + HK], ident[:],
                                         start=True, stop=True)
                elif item[0] == "bc":
                    hd = item[1]
                    pe.wait_ge(q["recip_ok"], 4 * (hd + 1))
                    last = pe.matmul(a[0:HD, :], ones_row[HD:HK, :], o_raw[HD:HK, :], start=True, stop=True)
                last.then_inc(aux_filled[pair], 1)
                if item[0] == "q" and item[1] + 2 < KV:
                    pe.wait_ge(aux_filled[pair], aux_of(item)[1] + 1)
                    pe.sem_inc(q["wq_free"], 1)

            start_aux(("xT",))
            pe.wait_ge(q["wk_split"], 1)
            n = 0
            for j in range(NCH):
                lo, hi = chunk_cols(j)
                w = hi - lo
                hh, hl = HH[j % 2], HL[j % 2]
                if j == 0:
                    pe.wait_ge(q["tail_low"], 1)
                else:
                    pe.wait_ge(q["ctx_split"], 2 * j)
                for part in range(kv_parts(j)):
                    if n >= 4:
                        pe.wait_ge(q["kv_free"], n - 3)
                    dst = banks[n % 4]
                    if part < 2:
                        for m in range(2):
                            h = 2 * part + m
                            for k4 in range(KD):
                                last = mm3(dst[0:HD, m * w:(m + 1) * w],
                                           WKH[:, k4, h * HD:(h + 1) * HD], WKL[:, k4, h * HD:(h + 1) * HD],
                                           hh[:, k4, 0:w], hl[:, k4, 0:w], k4 == 0, k4 == KD - 1)
                    else:
                        if n == 2:
                            pe.wait_ge(q["wv_split"], 1)
                        c = slice((part - 2) * P, (part - 1) * P)
                        for k4 in range(KD):
                            last = mm3(dst[:, 0:KV * HD], hh[:, k4, c], hl[:, k4, c],
                                       WVH[:, k4, :], WVL[:, k4, :], k4 == 0, k4 == KD - 1)
                    last.then_inc(q["kv_filled"], 1)
                    n += 1
                if j == NCH - 1:
                    pe.wait_ge(q["kv_filled"], n)
                    pe.sem_inc(q["proj_done"], 1)
                for item in pre[j]:
                    start_aux(item)
            pe.wait_ge(q["kv_free"], n)
            pe.wait_ge(q["pads"], 5)

            def project_out(hd):
                pe.wait_ge(q["on_ok"], hd + 1)
                pe.wait_ge(q[f"wo_in{hd % 2}"], 16 * (hd // 2 + 1))
                for g in range(G):
                    last = pe.matmul(banks[3][:, :], o_n[:, g * T:(g + 1) * T], WO[hd % 2][:, g, :],
                                     start=(hd == 0 and g == 0), stop=(hd == KV - 1 and g == G - 1))
                last.then_inc(q["o_proj"], 1)

            for s in range(NT + LAG + 8):
                h, t = s // KT, s % KT
                if s < NT:
                    if t == 0:
                        pair, k = aux_of(("nm", h))
                        pe.wait_ge(aux_free[pair], k + 1)
                    if s >= 2:
                        pe.wait_ge(q["exp_ok"], s - 1)
                    kc = slice(t * P, (t + 1) * P)
                    mm3(banks[s % 2][:, :], KH[:, h, kc], KL[:, h, kc], QH[:, h, :], QL[:, h, :],
                        True, True).then_inc(q["s_filled"], 1)
                for item in step_extra[s]:
                    start_aux(item)
                v = s - LAG
                if 0 <= v < NT:
                    hd, t = v // KT, v % KT
                    pe.wait_ge(*low_part(v))
                    if t == 0 and hd >= 1:
                        pe.wait_ge(q["o_raw_ok"], hd)
                    last = mm3(banks[2][0:HK, :], VH[:, hd, t, 0:HK], VL[:, hd, t, 0:HK],
                               PH[v % 4][:], PL[v % 4][:], t == 0, t == KT - 1)
                    last.then_inc(q["pv_ok"], 1)
                    if t == KT - 1:
                        pe.wait_ge(q["pv_ok"], v + 1)
                        pe.sem_inc(q["head_done"], 1)
                if s - LAG - KT >= 0 and (s - LAG - KT) % KT == 5:
                    project_out((s - LAG - KT) // KT)

            def transposes(k, done):
                pe.wait_ge(q["xn_ok"], k + 1)
                for k4 in range(KD):
                    last = pe.transpose(banks[4][:, k4 * T:(k4 + 1) * T], x_n[:, k4 * P:(k4 + 1) * P], ident[:])
                last.then_inc(q[done], 1)

            transposes(1, "x2T_tr")
            pe.wait_ge(q["x2T_ok"], 1)
            for part, (w_in, s_in, done) in enumerate(((w_inu, "winu_in", "u_filled"), (w_ing, "wing_in", "g_filled"))):
                pe.wait_ge(q[s_in], 16)
                for i in range(DT):
                    for k4 in range(KD):
                        last = pe.matmul(banks[2 * part + i // 4][:, (i % 4) * T:(i % 4 + 1) * T],
                                         w_in[:, k4, i * P:(i + 1) * P], x_T[:, k4, :],
                                         start=(k4 == 0), stop=(k4 == KD - 1))
                    if i % 4 == 3:
                        last.then_inc(q[done], 1)
            pe.wait_ge(q["wx_in"], 48)
            for i in range(DT):
                pe.wait_ge(q["u_ok"], i // 4 + 1)
                last = pe.matmul(banks[4][:, 0:R + 2 * N], u_c[:, i, :], w_x[:, i, :], start=(i == 0), stop=(i == DT - 1))
            last.then_inc(q["ssm_filled"], 1)
            pe.wait_ge(q["spn_ok"], 3)
            pe.transpose(banks[5][0:R + 2 * N, 0:T], sp[:], ident[:]).then_inc(q["tr_filled"], 1)
            pe.wait_ge(q["dtbc_ok"], 3)
            for i in range(DT):
                last = pe.matmul(banks[6 + i // 4][:, (i % 4) * T:(i % 4 + 1) * T], w_dt[:, i * P:(i + 1) * P],
                                 dt_t[:], start=True, stop=True)
                if i % 4 == 3:
                    last.then_inc(q["delta_filled"], 1)
            for k in range(8):
                if k >= 4:
                    pe.wait_ge(q["bb_ok"], k - 3)
                for m in range(4):
                    row = R + 4 * k + m
                    last = pe.matmul(banks[(0, 1, 4, 5)[k % 4]][:, m * T:(m + 1) * T],
                                     ident[R:R + 2 * N, row:row + 1].to_broadcast([2 * N, P]), bc_t[R:R + 2 * N, :],
                                     start=True, stop=True)
                last.then_inc(q["bb_filled"], 1)

            def mamba_out(i):
                pe.wait_ge(q["y2_ok"], i + 1)
                if i == 0:
                    pe.wait_ge(q["graw_ok"], 2)
                    pe.wait_ge(q["wout_in"], 16)
                last = pe.matmul(banks[2][:, :], y2[i % 2][:], w_out[:, i, :], start=(i == 0), stop=(i == DT - 1))
                last.then_inc(q["y2_used"], 1)

            pe.wait_ge(q["delta_ok"], 2)
            for i in range(DT):
                pe.wait_ge(q["yc_ok"], i + 1)
                if i >= 2:
                    pe.wait_ge(q["y1_ok"], i - 1)
                for m in range(N):
                    last = pe.matmul(banks[6 + i % 2][:, 0:T], ident[:], dBu[i % 2][:, m, :],
                                     start=(m == 0), stop=(m == N - 1))
                last.then_inc(q["y_filled"], 1)
                if i >= 1:
                    mamba_out(i - 1)
            mamba_out(DT - 1)
            pe.wait_ge(q["y2_used"], DT)
            pe.sem_inc(q["mo_filled"], 1)
            def down(m):
                pe.wait_ge(q["h_part"], m + 1)
                for i in range(GI * m, min(GI * m + GI, IT)):
                    w = w_dn[:, i, :] if i < IT - 1 else w_dnx[:, 0, :]
                    last = pe.matmul(banks[5][:, :], h_T[:, i, :], w, start=(i == 0), stop=(i == IT - 1))
                if m == ffn_groups() - 1:
                    last.then_inc(q["down_filled"], 1)

            transposes(2, "x3T_tr")
            pe.wait_ge(q["x3T_ok"], 1)
            pe.wait_ge(q["deq_ok"], sum(len(units_of(h)) for h in range(KV)))
            for m in range(ffn_groups()):
                if m >= 2:
                    pe.wait_ge(q["h_part"], m - 1)
                for side, w in enumerate((w_gate, w_up)):
                    for c in range(min(GI, IT - GI * m)):
                        i = GI * m + c
                        for k4 in range(KD):
                            last = pe.matmul(banks[2 * (m % 2) + side][:, c * T:(c + 1) * T],
                                             w[:, k4, i * P:(i + 1) * P], x_T[:, k4, :],
                                             start=(k4 == 0), stop=(k4 == KD - 1))
                last.then_inc(q["gu_filled"], 1)
                if m >= 1:
                    down(m - 1)
            down(ffn_groups() - 1)


def ffn_groups():
    return (IT + GI - 1) // GI


def kv_parts(j):
    return 3 if j == 0 else 2 + CH // P


def kv_items_upto(j):
    return sum(kv_parts(i) for i in range(j + 1))


def down_tiles(h):
    lo = (h * KT * VW) // D
    hi = ((h + 1) * KT * VW) // D
    return lo, (IT if h == KV - 1 else hi)


def units_of(h):
    u = [(k, h, c) for k in ("gate", "up") for c in range(I // ZU)]
    lo, hi = down_tiles(h)
    return u + [("down", i, c) for i in range(lo, hi) for c in range(D // ZU)]


def kernel(**inputs):
    import numpy as np
    import concourse.bacc as bacc
    from concourse.bass_utils import run_bass_kernel_spmd

    def rows(a, parts=P):
        return np.ascontiguousarray(a.reshape(-1, parts, a.shape[-1]).transpose(1, 0, 2))

    v = {k: np.asarray(a) for k, a in inputs.items()}
    m = {k[8:] if k.startswith("L0_attn_") else k: a for k, a in v.items()}
    data = {
        "x": v["x"][0],
        "ctx": rows(v["ctx_4096"][0].T),
        "wq": rows(v["L0_xattn_Wq"].T),
        "wk": rows(v["L0_xattn_Wk"].T),
        "wv": rows(v["L0_xattn_Wv"].T),
        "wo": rows(v["L0_xattn_Wo"].T, HD),
        "w_in": rows(m["W_in"].T),
        "conv_w": rows(m["conv_w"]),
        "conv_b": m["conv_b"].reshape(DT, P).T,
        "a": rows(m["A"]),
        "d": m["D_param"].reshape(DT, P).T,
        "ln_dt": m["dt_ln_w"].reshape(R, 1),
        "ln_b": m["b_ln_w"].reshape(N, 1),
        "ln_c": m["c_ln_w"].reshape(N, 1),
        "w_x": rows(m["Wx"].T),
        "w_dt": m["Wdt"].T,
        "dt_bias": m["dt_bias"].reshape(1, DI),
        "w_out": rows(m["W_out"].T),
        "gate_w": rows(v["L0_ffn_gate_w"]),
        "up_w": rows(v["L0_ffn_up_w"]),
        "down_w": rows(v["L0_ffn_down_w"]),
        "gate_z": v["L0_ffn_gate_z"], "gate_s": v["L0_ffn_gate_s"],
        "up_z": v["L0_ffn_up_z"], "up_s": v["L0_ffn_up_s"],
        "down_z": v["L0_ffn_down_z"], "down_s": v["L0_ffn_down_s"],
    }
    nc = bacc.Bacc("TRN2", target_bir_lowering=False, num_devices=1)
    arrays, aps = {}, {}
    for name, a in data.items():
        a = np.ascontiguousarray(a)
        arrays["in_" + name] = a
        aps[name] = nc.dram_tensor("in_" + name, a.shape, mybir.dt.from_np(a.dtype), kind="ExternalInput").ap()
    out = nc.dram_tensor("y", (T, D), F32, kind="ExternalOutput").ap()
    build(nc, aps, out)
    r = run_bass_kernel_spmd(nc, [arrays], core_ids=[0])
    return r.results[0]["y"].reshape(1, T, D)
```

```python
from contextlib import ExitStack

import concourse.bass as bass
from concourse import mybir

F32 = mybir.dt.float32
F32R = mybir.dt.float32r
I32 = mybir.dt.int32
ALU = mybir.AluOpType
ACT = mybir.ActivationFunctionType
AX_X = mybir.AxisListType.X

P = 128
T = 128
D = 512
KD = D // P
CTX = 2048
S = CTX + T
KV, G, HD = 4, 4, 96
HK = HD + 1
VW = HD + 2
CH = 256
NCH = 1 + CTX // CH
KT = S // P
NT = KV * KT
LAG = 3
DV = 4
DI = 1024
DT = DI // P
N = 16
R = 32
TAPS = 4
I = 1792
IT = I // P
GI = 4
ZC = 448
SCALE = float(HD) ** -0.5
LN_EPS = 1e-5
RMS_EPS = 1e-6


def chunk_cols(j):
    return (CTX, CTX + T) if j == 0 else ((j - 1) * CH, j * CH)


def build(nc, A, out):
    with ExitStack() as ctx:
        count = [0]

        def sem(name):
            return ctx.enter_context(nc.semaphore(name))

        def bank(name):
            return ctx.enter_context(nc.psum_tensor(name, [P, 512], F32))

        def at(offset, name, shape, dt=F32):
            with ExitStack() as hold:
                if offset:
                    count[0] += 1
                    hold.enter_context(nc.sbuf_tensor(f"skip{count[0]}", [P, offset // 4], F32))
                return hold.enter_context(nc.sbuf_tensor(name, shape, dt))

        class Row:
            def __init__(self, start):
                self.at = start

            def put(self, name, shape, dt=F32):
                n = 4
                for s in shape[1:]:
                    n *= s
                t = at(self.at, name, shape, dt)
                self.at += (n + 31) // 32 * 32
                return t

        fixed = Row(0)
        x_res = fixed.put("x_res", [P, D])
        x_n = fixed.put("x_n", [P, D])
        ident = fixed.put("ident", [P, P])
        conv_w = fixed.put("conv_w", [P, DT, TAPS])
        conv_b = fixed.put("conv_b", [P, DT])
        a_par = fixed.put("a_par", [P, DT, N])
        d_par = fixed.put("d_par", [P, DT])
        ln_w = fixed.put("ln_w", [R + 2 * N, 1])
        stats = fixed.put("stats", [P, 8])
        norm = fixed.put("norm", [P, 8])
        eps = fixed.put("eps", [P, 2])
        neg_max = fixed.put("neg_max", [P, HD + KV * G])
        part_max = fixed.put("part_max", [P, G, NCH])
        ones_row = fixed.put("ones_row", [P, HD])
        ident_r = fixed.put("ident_r", [P, P], F32R)
        zs = fixed.at
        x_nT = at(zs, "x_nT", [P, KD, T])
        k_at = zs + 4096

        keys = Row(k_at)
        KH = keys.put("KH", [HK, KV, S], F32R)
        kl_at = keys.at
        KL = keys.put("KL", [HK, KV, S], F32R)
        vh_at = keys.at
        VH = keys.put("VH", [P, KV, KT, VW], F32R)
        vl_at = keys.at
        VL = keys.put("VL", [P, KV, KT, VW], F32R)
        q_at = keys.at
        QH = keys.put("QH", [HK, KV, G * T], F32R)
        QL = keys.put("QL", [HK, KV, G * T], F32R)
        r_at = keys.at
        ZB = D * 4
        z_b = [at(o, f"z_b{i}", [P, D], I32) for i, o in enumerate((q_at, q_at + 4 * ZB, vl_at, q_at + 5 * ZB, q_at + 3 * ZB))]
        s_b = [at(o, f"s_b{i}", [P, D]) for i, o in enumerate((zs, zs + ZB, vl_at + ZB, vl_at, vl_at + 12 * ZB))]

        proj = Row(r_at)
        WKH, WKL, WVH, WVL = [proj.put(n, [P, KD, KV * HD], F32R) for n in ("WKH", "WKL", "WVH", "WVL")]
        HH = [proj.put(f"HH{i}", [P, KD, CH], F32R) for i in range(2)]
        HL = [proj.put(f"HL{i}", [P, KD, CH], F32R) for i in range(2)]
        c_raw = [proj.put(f"c_raw{i}", [P, KD, CH]) for i in range(2)]
        w_raw = [proj.put(f"w_raw{i}", [P, KD, KV * HD]) for i in range(2)]

        att = Row(r_at)
        PR = [att.put(f"PR{i}", [P, G * T]) for i in range(3)]
        PH = [att.put(f"PH{i}", [P, G * T], F32R) for i in range(4)]
        PL = [att.put(f"PL{i}", [P, G * T], F32R) for i in range(4)]
        WO = [att.put(f"WO{i}", [HD, G, D]) for i in range(2)]
        w_out = att.put("w_out", [P, DT, D])
        o_raw = att.put("o_raw", [HK, G * T])
        o_n = att.put("o_n", [HD, G * T])
        end_att = att.at

        w_gate = at(k_at, "w_gate", [P, KD, I])
        w_up = at(kl_at, "w_up", [P, KD, I])
        tail = KD * I * 4
        w_x = at(k_at + tail, "w_x", [P, DT, R + 2 * N])
        w_dt = at(k_at + tail + 2048, "w_dt", [R + 1, DI])
        w_dn = at(vh_at, "w_dn", [P, IT - 1, D])
        w_dnx = at(kl_at + tail, "w_dnx", [P, 1, D])
        w_inu = at(vl_at + ZB, "w_inu", [P, KD, DI])
        w_ing = at(r_at, "w_ing", [P, KD, DI])

        mam = Row(r_at + 2048)
        B_b = mam.put("B_b", [P, N, T])
        C_b = mam.put("C_b", [P, N, T])
        mid = mam.at
        dA = [mam.put(f"dA{i}", [P, N, T]) for i in range(2)]
        u_c = mam.put("u_c", [P, DT, T])
        assert mam.at <= r_at + 22528 + 16384
        delta = at(end_att - 4096, "delta", [P, DT, T])
        u_raw = at(mid, "u_raw", [P, DT, T])
        sig = at(mid + 8192, "sig", [P, DT, T])
        dBu = [at(o, f"dBu{i}", [P, N, T]) for i, o in enumerate((vl_at, vl_at + 8192, q_at + 10240))]
        du = at(vl_at + 16384, "du", [P, DT, T])
        g_s = at(vl_at + 20480, "g_s", [P, DT, T])
        x_T = x_n[:, :].rearrange("p (k t) -> p k t", k=KD)
        small = Row(q_at + 2048)
        sp = small.put("sp", [P, R + 2 * N])
        sq = small.put("sq", [P, R + 2 * N])
        dt_t = small.put("dt_t", [R + 1, T])
        bc_t = small.put("bc_t", [R + 2 * N, T])
        bc_h = small.put("bc_h", [R + 2 * N, T], F32R)
        bc_l = small.put("bc_l", [R + 2 * N, T], F32R)
        y2 = [at(q_at + 2048 + 512 * i, f"y2{i}", [P, T]) for i in range(2)]
        y1 = [at(q_at + 3072 + 512 * i, f"y1{i}", [P, T]) for i in range(2)]

        ffn = Row(r_at)
        f_sig = [ffn.put(f"f_sig{i}", [P, GI * T]) for i in range(2)]
        h_T = ffn.put("h_T", [P, IT, T])
        y_out = ffn.put("y_out", [P, D])

        banks = [bank(f"bank{i}") for i in range(8)]
        aux = [[banks[4], banks[5]], [banks[6], banks[7]]]

        names = (
            "x_in wk_in wv_in wo_in0 wo_in1 wout_in winu_in wing_in wx_in par_in ctx_in0 ctx_in1 wq_in0 wq_in1 "
            "z_in0 z_in1 z_in2 wgate_in wup_in wdn_in out_done "
            "consts pads stat_ok rstd_ok xn_ok wk_split wv_split ctx_split wraw_free wq_free raw_free "
            "kv_filled kv_high kv_free aux_filled0 aux_filled1 aux_free0 aux_free1 q_high xT_copy xT_high tail_low "
            "proj_done q_ok max_ok negmax_ok s_filled exp_ok ph_ok pl_pool pl_dve pv_ok head_done o_raw_ok recip_ok on_ok bc_last ident_ok "
            "o_proj x1_ok deq_sub deq_pool deq_dve x2T_tr x2T_ok u_filled g_filled uraw_ok conv_a conv_ok sil_a u_ok gsil_a gs_ok "
            "ssm_filled sp_ok ss_ok rms_ok spn_ok tr_filled dtbc_ok bc_low delta_filled dl_a delta_ok du_ok "
            "bb_filled bb_act bb_dve zero_ok dA_ok dBu_dve dBu_pool scan_ok yc_ok y_filled y1_ok y2_ok y2_used mo_filled x2_ok x3T_tr x3T_ok "
            "gu_filled fs_a h_part h_ok gu_free down_filled fin_ok act_seq dve_seq"
        ).split()
        q = {n: sem(n) for n in names}
        aux_filled = [q["aux_filled0"], q["aux_filled1"]]
        aux_free = [q["aux_free0"], q["aux_free1"]]

        aux_items = []
        step_extra = {}

        def add_aux(item):
            aux_items.append(item)

        pre = {}
        pre[0] = [("q", 0)]
        for j in range(1, NCH):
            pre[j] = [("mx", 0, j - 1)]
            if j in (1, 3, 5):
                pre[j].append(("q", (j + 1) // 2))
        pre[NCH - 1] += [("mx", 0, NCH - 1), ("nm", 0)]
        for step in range(NT + LAG):
            todo = []
            h, t = step // KT, step % KT
            if h + 1 < KV:
                todo += [("mx", h + 1, j) for j in range(NCH) if t == 3 * j // 2]
                if t == 15:
                    todo.append(("nm", h + 1))
            if h >= 1 and t == LAG + 4:
                todo.append(("bc", h - 1))
            step_extra[step] = todo
        add_aux(("xT",))
        for j in range(NCH):
            for it in pre[j]:
                add_aux(it)
        for step in range(NT + LAG):
            for it in step_extra[step]:
                add_aux(it)
        aux_index = {it: i for i, it in enumerate(aux_items)}

        def aux_of(item):
            i = aux_index[item]
            return i % 2, i // 2

        def piece(kind, g, c):
            if kind == "down":
                return w_dn[:, g, :] if g < IT - 1 else w_dnx[:, 0, :]
            return (w_gate if kind == "gate" else w_up)[:, g, c * ZC:(c + 1) * ZC]

        units = [u for h in range(KV) for u in units_of(h)]
        owner = [h for h in range(KV) for _ in units_of(h)]

        def zeros_at(u):
            return z_b[u % 3 if u % 3 < 2 else (2, 3, 3, 4)[owner[u]]]

        def scales_at(u):
            return s_b[u % 3 if u % 3 < 2 else (2, 3, 3, 4)[owner[u]]]

        def scaled(u):
            kinds = [units[i][0] == "down" for i in range(u + 1)]
            if kinds[-1]:
                return q["deq_dve"], sum(kinds)
            return q["deq_pool"], len(kinds) - sum(kinds)

        def deq_at(s):
            h, t = s // KT, s % KT
            return (1 + (t in (12, 14))) * int(h >= 1 and t >= 8) if h < KV else 0

        def low_part(s):
            if s % DV == 2:
                return q["pl_dve"], s // DV + 1
            return q["pl_pool"], s + 1 - (s + DV - 2) // DV

        def bcast(k):
            return ((B_b if k < 4 else C_b)[:, 4 * (k % 4):4 * (k % 4) + 4, :],
                    banks[(0, 1, 4, 5)[k % 4]][:, :].rearrange("p (i t) -> p i t", i=4))

        block = ctx.enter_context(nc.Block())

        @block.sync
        def _(sp_q):
            def load(dst, src, s):
                sp_q.dma_start(dst, src).then_inc(q[s], 16)

            load(x_res[:], A["x"], "x_in")
            load(w_raw[0][:], A["wk"], "wk_in")
            load(c_raw[0][:], A["ctx"][:, :, 0:CH], "ctx_in0")
            load(w_raw[1][:], A["wv"], "wv_in")
            load(c_raw[1][:], A["ctx"][:, :, CH:2 * CH], "ctx_in1")
            nq = 0
            for j in range(1, NCH):
                if nq < KV:
                    if nq < 2:
                        sp_q.wait_ge(q["wraw_free"], nq + 1)
                    else:
                        sp_q.wait_ge(q["wq_free"], nq - 1)
                    load(w_raw[nq % 2][:], A["wq"][:, :, nq * G * HD:(nq + 1) * G * HD], f"wq_in{nq % 2}")
                    nq += 1
                if j + 2 < NCH:
                    sp_q.wait_ge(q["raw_free"], j)
                    load(c_raw[(j + 1) % 2][:], A["ctx"][:, :, (j + 1) * CH:(j + 2) * CH], f"ctx_in{(j + 1) % 2}")
            load(conv_w[:], A["conv_w"], "par_in")
            load(conv_b[:], A["conv_b"], "par_in")
            load(a_par[:], A["a"], "par_in")
            load(d_par[:], A["d"], "par_in")
            load(ln_w[0:R, :], A["ln_dt"], "par_in")
            load(ln_w[R:R + N, :], A["ln_b"], "par_in")
            load(ln_w[R + N:R + 2 * N, :], A["ln_c"], "par_in")
            sp_q.wait_ge(q["proj_done"], 1)
            load(WO[0][:], A["wo"][:, 0:G, :], "wo_in0")
            load(WO[1][:], A["wo"][:, G:2 * G, :], "wo_in1")
            load(w_out[:], A["w_out"], "wout_in")
            unit = 0

            def load_unit():
                nonlocal unit
                if unit >= 3:
                    sp_q.wait_ge(*scaled(unit - 3))
                kind, g, c = units[unit]
                n = D if kind == "down" else ZC
                for dst, src in ((zeros_at(unit), A[kind + "_z"]), (scales_at(unit), A[kind + "_s"])):
                    load(dst[:, 0:n], src[g:g + 1, c * n:(c + 1) * n].to_broadcast([P, n]), f"z_in{unit % 3}")
                unit += 1

            for h in range(KV):
                sp_q.wait_ge(q["head_done"], h + 1)
                if h == KV - 1:
                    load(w_ing[:], A["w_in"][:, :, DI:2 * DI], "wing_in")
                    load(w_x[:], A["w_x"], "wx_in")
                    load(w_dt[0:R, :], A["w_dt"], "wx_in")
                    load(w_dt[R:R + 1, :], A["dt_bias"], "wx_in")
                load(w_gate[:, h, :].bitcast(I32), A["gate_w"][:, h, :], "wgate_in")
                for _ in range(3):
                    load_unit()
                load(w_up[:, h, :].bitcast(I32), A["up_w"][:, h, :], "wup_in")
                lo, hi = down_tiles(h)
                load(w_dn[:, lo:min(hi, IT - 1), :].bitcast(I32), A["down_w"][:, lo:min(hi, IT - 1), :], "wdn_in")
                if hi == IT:
                    load(w_dnx[:].bitcast(I32), A["down_w"][:, IT - 1:IT, :], "wdn_in")
                if h == KV - 2:
                    load(w_inu[:], A["w_in"][:, :, 0:DI], "winu_in")
                while unit < len(units) and owner[unit] == h:
                    load_unit()
                if h + 2 < KV:
                    sp_q.wait_ge(q["o_proj"], h + 1)
                    load(WO[h % 2][:], A["wo"][:, (h + 2) * G:(h + 3) * G, :], f"wo_in{h % 2}")
            sp_q.wait_ge(q["fin_ok"], 1)
            sp_q.dma_start(out, y_out[:]).then_inc(q["out_done"], 16)
            sp_q.wait_ge(q["out_done"], 16)

        @block.gpsimd
        def _(pool):
            pool.memset(ident[:], 0.0).then_inc(q["zero_ok"], 1)
            pool.memset(eps[:, 0:1], LN_EPS)
            pool.memset(eps[:, 1:2], RMS_EPS)
            pool.memset(neg_max[:], 0.0)
            pool.memset(ones_row[:], 1.0)
            pool.wait_ge(q["zero_ok"], 1)
            pool.affine_select(out=ident[:], in_=ident[:], compare_op=ALU.not_equal, fill=1.0, base=0,
                               pattern=[[-1, P]], channel_multiplier=1).then_inc(q["consts"], 1)
            for j in range(1, NCH):
                b = (j - 1) % 2
                pool.wait_ge(q[f"ctx_in{b}"], 16 * ((j - 1) // 2 + 1))
                if j >= 2:
                    pool.wait_ge(q["kv_filled"], kv_items_upto(j - 2))
                pool.tensor_scalar(HH[j % 2][:], c_raw[b][:], 1.0, None, ALU.mult).then_inc(q["ctx_split"], 1)
                pool.wait_ge(q["ctx_split"], 2 * j - 1)
                pool.tensor_tensor(HL[j % 2][:], c_raw[b][:], HH[j % 2][:].bitcast(F32),
                                   ALU.subtract).then_inc(q["ctx_split"], 1)
                pool.wait_ge(q["ctx_split"], 2 * j)
                pool.sem_inc(q["raw_free"], 1)
                if j == 1:
                    for m, (cells, value) in enumerate(((KH[HD:HK, :, :], 1.0), (KL[HD:HK, :, :], 0.0),
                                                        (QL[HD:HK, :, :], 0.0), (VH[:, :, :, HD:VW], 1.0),
                                                        (VL[:, :, :, HD:VW], 0.0))):
                        pool.memset(cells.bitcast(F32), value).then_inc(q["pads"], 1)
                        pool.wait_ge(q["pads"], m + 1)
            unit = 0

            def scale_unit():
                nonlocal unit
                kind, g, c = units[unit]
                if kind != "down":
                    pool.wait_ge(q["deq_sub"], unit + 1)
                    w = piece(kind, g, c)
                    pool.tensor_tensor(w, w, scales_at(unit)[:, 0:ZC], ALU.mult).then_inc(q["deq_pool"], 1)
                unit += 1

            for s in range(NT):
                if s % DV != 2:
                    pool.wait_ge(q["ph_ok"], s + 1)
                    if s >= 4:
                        pool.wait_ge(q["pv_ok"], s - 3)
                    pool.tensor_tensor(PL[s % 4][:], PR[s % 3][:], PH[s % 4][:].bitcast(F32),
                                       ALU.subtract).then_inc(q["pl_pool"], 1)
                for _ in range(deq_at(s)):
                    scale_unit()
            while unit < len(units):
                scale_unit()
            pool.wait_ge(q["delta_ok"], 2)
            for b in range(2):
                last = pool.memset(dA[b][:, :, 0:1], 0.0)
            last.then_inc(q["zero_ok"], 1)
            pool.wait_ge(q["bb_act"], 2)
            pool.wait_ge(q["bb_dve"], 2)
            pool.wait_ge(q["du_ok"], 1)
            for i in range(1, DT):
                if i >= 3:
                    pool.wait_ge(q["y_filled"], i - 2)
                pool.tensor_tensor(dBu[i % 3][:], B_b[:], du[:, i:i + 1, :].to_broadcast([P, N, T]),
                                   ALU.mult).then_inc(q["dBu_pool"], 1)

        @block.scalar
        def _(act):
            def rstd(src, dst, e, scale=1.0):
                act.activation(dst, src, ACT.Ln, bias=e, scale=scale).then_inc(q["act_seq"], 1)
                seq[0] += 1
                act.wait_ge(q["act_seq"], seq[0])
                return act.activation(dst, dst, ACT.Exp, scale=-0.5)

            seq = [0]

            def chain(ins):
                ins.then_inc(q["act_seq"], 1)
                seq[0] += 1
                act.wait_ge(q["act_seq"], seq[0])

            act.preload_act_table_set("natural_log_exp_and_others")
            act.wait_ge(q["consts"], 1)
            act.wait_ge(q["stat_ok"], 1)
            rstd(stats[:, 7:8], norm[:, 0:1], eps[:, 0:1]).then_inc(q["rstd_ok"], 1)

            def evac_aux(item):
                pair, k = aux_of(item)
                act.wait_ge(aux_filled[pair], k + 1)
                src = aux[pair][0]
                if item[0] == "xT":
                    v = src[:, :].rearrange("p (k t) -> p k t", k=KD)
                    act.activation(x_nT[:], v, ACT.Copy).then_inc(q["xT_copy"], 1)
                    act.activation(HH[0][:, :, 0:T], v, ACT.Copy).then_inc(q["xT_high"], 1)
                elif item[0] == "q":
                    act.activation(QH[0:HD, item[1], :], src[0:HD, :], ACT.Copy).then_inc(q["q_high"], 1)
                elif item[0] == "nm":
                    act.activation(QH[HD:HK, item[1], :], src[HD:HK, :], ACT.Copy).then_inc(aux_free[pair], 1)

            evac_aux(("xT",))
            n = 0
            for j in range(NCH):
                lo, hi = chunk_cols(j)
                for part in range(kv_parts(j)):
                    act.wait_ge(q["kv_filled"], n + 1)
                    src = banks[n % 4]
                    if part < 2:
                        for dst, v in key_moves(KH, src, part, lo, hi):
                            last = act.activation(dst, v, ACT.Copy)
                        last.then_inc(q["kv_high"], 1)
                    else:
                        v = src[:, 0:KV * HD].rearrange("p (h d) -> p h d", h=KV)
                        act.activation(VH[:, :, lo // P + part - 2, 0:HD], v, ACT.Copy).then_inc(q["kv_high"], 1)
                    n += 1
                for item in pre[j]:
                    if item[0] in ("q", "nm"):
                        evac_aux(item)

            for s in range(NT + LAG):
                h, t = s // KT, s % KT
                if s < NT:
                    act.wait_ge(q["s_filled"], s + 1)
                    if s >= 3:
                        act.wait_ge(*low_part(s - 3))
                    elif s == 0:
                        act.wait_ge(q["proj_done"], 1)
                    act.activation(PR[s % 3][:], banks[s % 2][:, :], ACT.Exp, scale=SCALE).then_inc(q["exp_ok"], 1)
                    act.wait_ge(q["exp_ok"], s + 1)
                    if s >= 4:
                        act.wait_ge(q["pv_ok"], s - 3)
                    act.activation(PH[s % 4][:], PR[s % 3][:], ACT.Copy).then_inc(q["ph_ok"], 1)
                if s >= LAG and (s - LAG) % KT == KT - 1:
                    hd = (s - LAG) // KT
                    act.wait_ge(q["head_done"], hd + 1)
                    if hd >= 1:
                        act.wait_ge(q["on_ok"], hd)
                    act.activation(o_raw[:], banks[2][0:HK, :], ACT.Copy).then_inc(q["o_raw_ok"], 1)
                for item in step_extra[s]:
                    if item[0] == "nm":
                        evac_aux(item)

            act.wait_ge(q["stat_ok"], 2)
            rstd(stats[:, 7:8], norm[:, 0:1], eps[:, 0:1]).then_inc(q["rstd_ok"], 1)
            act.wait_ge(q["x2T_tr"], 1)
            act.activation(x_T, banks[4][:, :].rearrange("p (k t) -> p k t", k=KD), ACT.Copy).then_inc(q["x2T_ok"], 1)

            def sigmoid(dst, src):
                chain(act.activation(dst, src, ACT.Exp, scale=-1.0))
                chain(act.activation(dst, dst, ACT.Ln, bias=1.0))
                return act.activation(dst, dst, ACT.Exp, scale=-1.0)

            act.wait_ge(q["par_in"], 16 * 7)
            for half in range(2):
                tiles = range(4 * half, 4 * half + 4)
                act.wait_ge(q["u_filled"], half + 1)
                chain(act.activation(u_raw[:, 4 * half:4 * half + 4, :],
                                     banks[half][:, :].rearrange("p (i t) -> p i t", i=4), ACT.Copy))
                for i in tiles:
                    last = act.activation(u_c[:, i, :], u_raw[:, i, :], ACT.Identity,
                                          bias=conv_b[:, i:i + 1], scale=conv_w[:, i, TAPS - 1:TAPS])
                last.then_inc(q["conv_a"], 1)
            def gate_sigmoid(half):
                act.wait_ge(q["g_filled"], half + 1)
                sigmoid(g_s[:, 4 * half:4 * half + 4, :],
                        banks[2 + half][:, :].rearrange("p (i t) -> p i t", i=4)).then_inc(q["gsil_a"], 1)

            for half in range(2):
                sl = slice(4 * half, 4 * half + 4)
                act.wait_ge(q["conv_ok"], 4 * (half + 1))
                sigmoid(sig[:, sl, :], u_c[:, sl, :]).then_inc(q["sil_a"], 1)
                if half == 0:
                    gate_sigmoid(0)
            act.wait_ge(q["ssm_filled"], 1)
            act.activation(sp[:], banks[4][:, 0:R + 2 * N], ACT.Copy).then_inc(q["sp_ok"], 1)
            act.wait_ge(q["ss_ok"], 1)
            chain(act.activation(norm[:, 2:3], norm[:, 2:3], ACT.Ln, bias=eps[:, 1:2], scale=1.0 / R))
            chain(act.activation(norm[:, 3:5], norm[:, 3:5], ACT.Ln, bias=eps[:, 1:2], scale=1.0 / N))
            act.activation(norm[:, 2:5], norm[:, 2:5], ACT.Exp, scale=-0.5).then_inc(q["rms_ok"], 1)
            act.wait_ge(q["tr_filled"], 1)
            act.activation(dt_t[0:R, :], banks[5][0:R, 0:T], ACT.Copy, scale=ln_w[0:R, :]).then_inc(q["dtbc_ok"], 1)
            for dst in (bc_t, bc_h):
                act.activation(dst[R:R + 2 * N, :], banks[5][R:R + 2 * N, 0:T], ACT.Copy,
                               scale=ln_w[R:R + 2 * N, :]).then_inc(q["dtbc_ok"], 1)
            gate_sigmoid(1)
            for half in range(2):
                sl = slice(4 * half, 4 * half + 4)
                act.wait_ge(q["delta_filled"], half + 1)
                z = banks[6 + half][:, :].rearrange("p (i t) -> p i t", i=4)
                chain(act.activation(sig[:, sl, :], z, ACT.Abs))
                chain(act.activation(sig[:, sl, :], sig[:, sl, :], ACT.Exp, scale=-1.0))
                act.activation(sig[:, sl, :], sig[:, sl, :], ACT.Ln, bias=1.0).then_inc(q["dl_a"], 1)
            for k in range(2):
                act.wait_ge(q["bb_filled"], k + 1)
                dst, src = bcast(k)
                act.activation(dst, src, ACT.Copy).then_inc(q["bb_act"], 1)
            act.wait_ge(q["delta_ok"], 2)
            act.wait_ge(q["zero_ok"], 2)
            for i in range(DT):
                if i >= 2:
                    act.wait_ge(q["scan_ok"], i - 1)
                for m in range(N):
                    last = act.activation(dA[i % 2][:, m, 1:T], delta[:, i, 1:T], ACT.Exp, scale=a_par[:, i, m:m + 1])
                last.then_inc(q["dA_ok"], 1)
            act.wait_ge(q["stat_ok"], 3)
            rstd(stats[:, 7:8], norm[:, 0:1], eps[:, 0:1]).then_inc(q["rstd_ok"], 1)
            act.wait_ge(q["x3T_tr"], 1)
            act.activation(x_T, banks[4][:, :].rearrange("p (k t) -> p k t", k=KD), ACT.Copy).then_inc(q["x3T_ok"], 1)
            for m in range(ffn_groups()):
                n = min(GI, IT - GI * m) * T
                act.wait_ge(q["gu_filled"], m + 1)
                if m >= 2:
                    act.wait_ge(q["h_part"], m - 1)
                sigmoid(f_sig[m % 2][:, 0:n], banks[2 * (m % 2)][:, 0:n]).then_inc(q["fs_a"], 1)

        @block.vector
        def _(dve):
            seq = [0]

            def chain(ins):
                ins.then_inc(q["dve_seq"], 1)
                seq[0] += 1
                dve.wait_ge(q["dve_seq"], seq[0])

            def norm_rows(k):
                chain(dve.bn_stats(stats[:, 0:6], x_res[:]))
                dve.bn_aggr(stats[:, 6:8], stats[:, 0:6]).then_inc(q["stat_ok"], 1)
                dve.wait_ge(q["stat_ok"], k + 1)
                dve.wait_ge(q["rstd_ok"], k + 1)
                dve.tensor_scalar(x_n[:], x_res[:], stats[:, 6:7], norm[:, 0:1],
                                  ALU.subtract, ALU.mult).then_inc(q["xn_ok"], 1)

            dve.wait_ge(q["x_in"], 16)
            norm_rows(0)
            dve.wait_ge(q["consts"], 1)
            dve.tensor_copy(ident_r[:], ident[:]).then_inc(q["ident_ok"], 1)
            dve.wait_ge(q["wk_in"], 16)
            chain(dve.tensor_copy(WKH[:], w_raw[0][:]))
            dve.tensor_tensor(WKL[:], w_raw[0][:], WKH[:].bitcast(F32), ALU.subtract).then_inc(q["wk_split"], 1)
            pair, k = aux_of(("xT",))
            dve.wait_ge(q["xT_high"], 1)
            dve.tensor_tensor(HL[0][:, :, 0:T], aux[pair][0][:, :].rearrange("p (k t) -> p k t", k=KD),
                              HH[0][:, :, 0:T].bitcast(F32), ALU.subtract).then_inc(q["tail_low"], 1)
            dve.wait_ge(q["tail_low"], 1)
            dve.sem_inc(aux_free[pair], 1)
            dve.wait_ge(q["wk_split"], 1)
            dve.sem_inc(q["wraw_free"], 1)
            dve.wait_ge(q["wv_in"], 16)
            chain(dve.tensor_copy(WVH[:], w_raw[1][:]))
            chain(dve.tensor_tensor(WVL[:], w_raw[1][:], WVH[:].bitcast(F32), ALU.subtract))
            dve.sem_inc(q["wv_split"], 1)
            dve.sem_inc(q["wraw_free"], 1)

            def take_aux(item):
                pair, k = aux_of(item)
                a, b = aux[pair]
                dve.wait_ge(aux_filled[pair], k + 1)
                if item[0] == "q":
                    h = item[1]
                    dve.wait_ge(q["q_high"], h + 1)
                    dve.tensor_tensor(QL[0:HD, h, :], a[0:HD, :], QH[0:HD, h, :].bitcast(F32),
                                      ALU.subtract).then_inc(aux_free[pair], 1)
                elif item[0] == "mx":
                    _, h, j = item
                    lo, hi = chunk_cols(j)
                    w = hi - lo
                    for m, bk in enumerate((a, b)):
                        last = dve.tensor_reduce(part_max[:, 2 * m:2 * m + 2, j],
                                                 bk[:, 0:2 * w].rearrange("p (g t) -> p g t", g=2), AX_X, ALU.max)
                    last.then_inc(aux_free[pair], 1)
                    if j == NCH - 1:
                        dve.wait_ge(aux_free[pair], k + 1)
                        dve.tensor_reduce(neg_max[:, HD + G * h:HD + G * (h + 1)], part_max[:], AX_X, ALU.max,
                                          negate=True).then_inc(q["max_ok"], 1)
                        dve.wait_ge(q["max_ok"], h + 1)

            def bc_take(hd):
                pair, k = aux_of(("bc", hd))
                dve.wait_ge(aux_filled[pair], k + 1)
                if hd >= 1:
                    dve.wait_ge(q["o_proj"], hd)
                dve.tensor_tensor(o_n[:], o_raw[0:HD, :], aux[pair][0][0:HD, :], ALU.mult).then_inc(q["on_ok"], 1)
                dve.wait_ge(q["on_ok"], hd + 1)
                dve.sem_inc(aux_free[pair], 1)

            def recip(g):
                cols = slice(g * T, (g + 1) * T)
                dve.reciprocal(o_raw[HD:HK, cols], o_raw[HD:HK, cols]).then_inc(q["recip_ok"], 1)

            unit = 0

            def zero_unit():
                nonlocal unit
                kind, g, c = units[unit]
                h = owner[unit]
                loads = h + 1 if (kind, g) != ("down", IT - 1) else KV + 1
                dve.wait_ge(q[{"gate": "wgate_in", "up": "wup_in", "down": "wdn_in"}[kind]], 16 * loads)
                dve.wait_ge(q[f"z_in{unit % 3}"], 32 * (unit // 3 + 1))
                w = piece(kind, g, c)
                n = D if kind == "down" else ZC
                dve.tensor_tensor(w, w.bitcast(I32), zeros_at(unit)[:, 0:n], ALU.subtract).then_inc(q["deq_sub"], 1)
                if kind == "down":
                    dve.wait_ge(q["deq_sub"], unit + 1)
                    dve.tensor_tensor(w, w, scales_at(unit)[:], ALU.mult).then_inc(q["deq_dve"], 1)
                unit += 1

            n = 0
            for j in range(NCH):
                lo, hi = chunk_cols(j)
                for part in range(kv_parts(j)):
                    dve.wait_ge(q["kv_high"], n + 1)
                    src = banks[n % 4]
                    if part < 2:
                        for (dst, v), (high, _) in zip(key_moves(KL, src, part, lo, hi), key_moves(KH, src, part, lo, hi)):
                            last = dve.tensor_tensor(dst, v, high.bitcast(F32), ALU.subtract)
                        last.then_inc(q["kv_free"], 1)
                    else:
                        v = src[:, 0:KV * HD].rearrange("p (h d) -> p h d", h=KV)
                        kt = lo // P + part - 2
                        dve.tensor_tensor(VL[:, :, kt, 0:HD], v, VH[:, :, kt, 0:HD].bitcast(F32),
                                          ALU.subtract).then_inc(q["kv_free"], 1)
                    n += 1
                for item in pre[j]:
                    take_aux(item)

            dve.wait_ge(q["proj_done"], 1)
            for s in range(NT + LAG):
                h, t = s // KT, s % KT
                if s < NT and s % DV == 2:
                    dve.wait_ge(q["ph_ok"], s + 1)
                    if s >= 4:
                        dve.wait_ge(q["pv_ok"], s - 3)
                    dve.tensor_tensor(PL[s % 4][:], PR[s % 3][:], PH[s % 4][:].bitcast(F32),
                                      ALU.subtract).then_inc(q["pl_dve"], 1)
                for item in step_extra[s]:
                    if item[0] == "mx":
                        take_aux(item)
                fin = s - LAG - KT
                if fin >= 0 and fin % KT < G:
                    if fin % KT == 0:
                        dve.wait_ge(q["o_raw_ok"], fin // KT + 1)
                    recip(fin % KT)
                if fin >= 0 and fin % KT == G + 1:
                    bc_take(fin // KT)
                for _ in range(deq_at(s)):
                    zero_unit()
            dve.wait_ge(q["o_raw_ok"], KV)
            recip(0)
            for g in range(G):
                if g + 1 < G:
                    recip(g + 1)
                dve.wait_ge(q["bc_last"], g + 1)
                if g == 0:
                    dve.wait_ge(q["o_proj"], KV - 1)
                cols = slice(g * T, (g + 1) * T)
                dve.tensor_tensor(o_n[:, cols], o_raw[0:HD, cols], banks[4 + g][0:HD, 0:T], ALU.mult).then_inc(q["on_ok"], 1)
            dve.wait_ge(q["o_proj"], KV)
            chain(dve.tensor_tensor(x_res[:], banks[3][:, :], x_res[:], ALU.add))
            norm_rows(1)
            for _ in range(3):
                zero_unit()
            for half in range(2):
                dve.wait_ge(q["conv_a"], half + 1)
                for shift in range(1, TAPS):
                    for i in range(4 * half, 4 * half + 4):
                        dve.scalar_tensor_tensor(u_c[:, i, shift:T], u_raw[:, i, 0:T - shift],
                                                 conv_w[:, i, TAPS - 1 - shift:TAPS - shift], u_c[:, i, shift:T],
                                                 ALU.mult, ALU.add).then_inc(q["conv_ok" if shift == TAPS - 1 else "dve_seq"], 1)
                        if shift < TAPS - 1:
                            seq[0] += 1
                    if shift < TAPS - 1:
                        dve.wait_ge(q["dve_seq"], seq[0])
            for half in range(2):
                sl = slice(4 * half, 4 * half + 4)
                dve.wait_ge(q["sil_a"], half + 1)
                dve.tensor_tensor(u_c[:, sl, :], u_c[:, sl, :], sig[:, sl, :], ALU.mult).then_inc(q["u_ok"], 1)
                zero_unit()
            dve.memset(dt_t[R:R + 1, :], 1.0).then_inc(q["dtbc_ok"], 1)
            dve.wait_ge(q["sp_ok"], 1)
            chain(dve.tensor_tensor(sq[:], sp[:], sp[:], ALU.mult))
            dve.tensor_reduce(norm[:, 2:3], sq[:, 0:R], AX_X, ALU.add)
            dve.tensor_reduce(norm[:, 3:5], sq[:, R:R + 2 * N].rearrange("p (a n) -> p a n", a=2), AX_X,
                              ALU.add).then_inc(q["ss_ok"], 1)
            dve.wait_ge(q["rms_ok"], 1)
            for a, (lo, hi) in enumerate(((0, R), (R, R + N), (R + N, R + 2 * N))):
                dve.tensor_scalar(sp[:, lo:hi], sp[:, lo:hi], norm[:, 2 + a:3 + a], None,
                                  ALU.mult).then_inc(q["spn_ok"], 1)
            dve.wait_ge(q["dtbc_ok"], 4)
            dve.tensor_tensor(bc_l[R:, :], bc_t[R:, :], bc_h[R:, :].bitcast(F32), ALU.subtract).then_inc(q["bc_low"], 1)
            for _ in range(3):
                zero_unit()
            for half in range(2):
                sl = slice(4 * half, 4 * half + 4)
                dve.wait_ge(q["dl_a"], half + 1)
                z = banks[6 + half][:, :].rearrange("p (i t) -> p i t", i=4)
                dve.scalar_tensor_tensor(delta[:, sl, :], z, 0.0, sig[:, sl, :], ALU.max, ALU.add).then_inc(q["delta_ok"], 1)
            dve.wait_ge(q["delta_ok"], 2)
            dve.tensor_tensor(du[:], delta[:], u_c[:], ALU.mult).then_inc(q["du_ok"], 1)
            for k in range(2, 8):
                dve.wait_ge(q["bb_filled"], k + 1)
                dst, src = bcast(k)
                dve.tensor_copy(dst, src).then_inc(q["bb_dve"], 1)
                if k == 3:
                    dve.wait_ge(q["du_ok"], 1)
                    dve.wait_ge(q["bb_act"], 2)
                    dve.wait_ge(q["bb_dve"], 2)
                    dve.tensor_tensor(dBu[0][:], B_b[:], du[:, 0:1, :].to_broadcast([P, N, T]),
                                      ALU.mult).then_inc(q["dBu_dve"], 1)
            dve.wait_ge(q["gsil_a"], 2)
            for half in range(2):
                sl = slice(4 * half, 4 * half + 4)
                dve.tensor_tensor(g_s[:, sl, :], g_s[:, sl, :], banks[2 + half][:, :].rearrange("p (i t) -> p i t", i=4),
                                  ALU.mult).then_inc(q["gs_ok"], 1)

            def gate_out(i):
                dve.wait_ge(q["y_filled"], i + 1)
                if i >= 2:
                    dve.wait_ge(q["y2_used"], i - 1)
                dve.scalar_tensor_tensor(y1[i % 2][:], u_c[:, i, :], d_par[:, i:i + 1], banks[6 + i % 2][:, 0:T],
                                         ALU.mult, ALU.add).then_inc(q["y1_ok"], 1)
                dve.wait_ge(q["y1_ok"], i + 1)
                dve.tensor_tensor(y2[i % 2][:], y1[i % 2][:], g_s[:, i, :], ALU.mult).then_inc(q["y2_ok"], 1)

            for i in range(DT):
                b = i % 2
                dve.wait_ge(q["dA_ok"], i + 1)
                dve.wait_ge(*((q["dBu_dve"], 1) if i == 0 else (q["dBu_pool"], i)))
                flat = dBu[i % 3][:].rearrange("p n t -> p (n t)")
                dve.tensor_tensor_scan(flat, dA[b][:].rearrange("p n t -> p (n t)"), flat, 0.0,
                                       ALU.mult, ALU.add).then_inc(q["scan_ok"], 1)
                dve.wait_ge(q["scan_ok"], i + 1)
                if i == 0:
                    dve.wait_ge(q["bb_dve"], 6)
                dve.tensor_tensor(dBu[i % 3][:], dBu[i % 3][:], C_b[:], ALU.mult).then_inc(q["yc_ok"], 1)
                if i == 0:
                    dve.wait_ge(q["gs_ok"], 2)
                else:
                    gate_out(i - 1)
            gate_out(DT - 1)
            dve.wait_ge(q["mo_filled"], 1)
            chain(dve.tensor_tensor(x_res[:], banks[2][:, :], x_res[:], ALU.add))
            norm_rows(2)
            while unit < len(units):
                zero_unit()
            for m in range(ffn_groups()):
                n = min(GI, IT - GI * m) * T
                dve.wait_ge(q["fs_a"], m + 1)
                hs = h_T[:, GI * m:GI * m + n // T, :].rearrange("p i t -> p (i t)")
                chain(dve.tensor_tensor(f_sig[m % 2][:, 0:n], banks[2 * (m % 2)][:, 0:n], f_sig[m % 2][:, 0:n], ALU.mult))
                dve.tensor_tensor(hs, banks[2 * (m % 2) + 1][:, 0:n], f_sig[m % 2][:, 0:n],
                                  ALU.mult).then_inc(q["h_part"], 1)
            dve.wait_ge(q["down_filled"], 1)
            dve.tensor_tensor(y_out[:], banks[5][:, :], x_res[:], ALU.add).then_inc(q["fin_ok"], 1)

        @block.tensor
        def _(pe):
            def mm3(dst, wh, wl, xh, xl, start, stop):
                pe.matmul(dst, wh, xh, start=start, stop=False)
                pe.matmul(dst, wh, xl, start=False, stop=False)
                return pe.matmul(dst, wl, xh, start=False, stop=stop)

            def start_aux(item):
                pair, k = aux_of(item)
                if k >= 1:
                    pe.wait_ge(aux_free[pair], k)
                a, b = aux[pair]
                if item[0] == "xT":
                    pe.wait_ge(q["xn_ok"], 1)
                    pe.wait_ge(q["consts"], 1)
                    for k4 in range(KD):
                        last = pe.transpose(a[:, k4 * T:(k4 + 1) * T], x_n[:, k4 * P:(k4 + 1) * P], ident[:])
                elif item[0] == "q":
                    h = item[1]
                    pe.wait_ge(q["xT_copy"], 1)
                    pe.wait_ge(q[f"wq_in{h % 2}"], 16 * (h // 2 + 1))
                    for g in range(G):
                        for k4 in range(KD):
                            last = pe.matmul(a[0:HD, g * T:(g + 1) * T], w_raw[h % 2][:, k4, g * HD:(g + 1) * HD],
                                             x_nT[:, k4, :], start=(k4 == 0), stop=(k4 == KD - 1))
                elif item[0] == "mx":
                    _, h, j = item
                    lo, hi = chunk_cols(j)
                    if h == 0:
                        pe.wait_ge(q["kv_high"], kv_items_upto(j - 1) + 1)
                    pe.wait_ge(q["q_high"], h + 1)
                    for g in range(G):
                        bk = (a, b)[g // 2]
                        w = hi - lo
                        last = pe.matmul(bk[:, (g % 2) * w:(g % 2 + 1) * w], QH[0:HD, h, g * T:(g + 1) * T],
                                         KH[0:HD, h, lo:hi], start=True, stop=True)
                elif item[0] == "nm":
                    h = item[1]
                    pe.wait_ge(q["max_ok"], h + 1)
                    for g in range(G):
                        c = G * h + g
                        last = pe.matmul(a[0:HK, g * T:(g + 1) * T], neg_max[:, c:c + HK], ident[:],
                                         start=True, stop=True)
                elif item[0] == "bc":
                    hd = item[1]
                    pe.wait_ge(q["recip_ok"], 4 * (hd + 1))
                    last = pe.matmul(a[0:HD, :], ones_row[HD:HK, :], o_raw[HD:HK, :], start=True, stop=True)
                last.then_inc(aux_filled[pair], 1)
                if item[0] == "q" and item[1] + 2 < KV:
                    pe.wait_ge(aux_filled[pair], aux_of(item)[1] + 1)
                    pe.sem_inc(q["wq_free"], 1)

            start_aux(("xT",))
            pe.wait_ge(q["wk_split"], 1)
            n = 0
            for j in range(NCH):
                lo, hi = chunk_cols(j)
                w = hi - lo
                hh, hl = HH[j % 2], HL[j % 2]
                if j == 0:
                    pe.wait_ge(q["tail_low"], 1)
                else:
                    pe.wait_ge(q["ctx_split"], 2 * j)
                for part in range(kv_parts(j)):
                    if n >= 4:
                        pe.wait_ge(q["kv_free"], n - 3)
                    dst = banks[n % 4]
                    if part < 2:
                        for m in range(2 - part):
                            c = slice((2 * part + m) * P, (2 * part + m + 1) * P)
                            for k4 in range(KD):
                                last = mm3(dst[:, m * w:(m + 1) * w], WKH[:, k4, c], WKL[:, k4, c],
                                           hh[:, k4, 0:w], hl[:, k4, 0:w], k4 == 0, k4 == KD - 1)
                    else:
                        if n == 2:
                            pe.wait_ge(q["wv_split"], 1)
                        c = slice((part - 2) * P, (part - 1) * P)
                        for k4 in range(KD):
                            last = mm3(dst[:, 0:KV * HD], hh[:, k4, c], hl[:, k4, c],
                                       WVH[:, k4, :], WVL[:, k4, :], k4 == 0, k4 == KD - 1)
                    last.then_inc(q["kv_filled"], 1)
                    n += 1
                if j == NCH - 1:
                    pe.wait_ge(q["kv_filled"], n)
                    pe.sem_inc(q["proj_done"], 1)
                for item in pre[j]:
                    start_aux(item)
            pe.wait_ge(q["kv_free"], n)
            pe.wait_ge(q["pads"], 5)

            def project_head(hd, g):
                pe.wait_ge(q["on_ok"], hd + g + 1)
                if g == 0:
                    pe.wait_ge(q[f"wo_in{hd % 2}"], 16 * (hd // 2 + 1))
                last = pe.matmul(banks[3][:, :], o_n[:, g * T:(g + 1) * T], WO[hd % 2][:, g, :],
                                 start=False, stop=(g == G - 1))
                if g == G - 1:
                    last.then_inc(q["o_proj"], 1)

            def project_out(hd):
                pe.wait_ge(q["on_ok"], hd + 1)
                pe.wait_ge(q[f"wo_in{hd % 2}"], 16 * (hd // 2 + 1))
                for g in range(G):
                    last = pe.matmul(banks[3][:, :], o_n[:, g * T:(g + 1) * T], WO[hd % 2][:, g, :],
                                     start=(hd == 0 and g == 0), stop=False)
                last.then_inc(q["o_proj"], 1)

            for s in range(NT + LAG):
                h, t = s // KT, s % KT
                if s < NT:
                    if t == 0:
                        pair, k = aux_of(("nm", h))
                        pe.wait_ge(aux_free[pair], k + 1)
                    if s >= 2:
                        pe.wait_ge(q["exp_ok"], s - 1)
                    kc = slice(t * P, (t + 1) * P)
                    mm3(banks[s % 2][:, :], KH[:, h, kc], KL[:, h, kc], QH[:, h, :], QL[:, h, :],
                        True, True).then_inc(q["s_filled"], 1)
                for item in step_extra[s]:
                    start_aux(item)
                v = s - LAG
                if 0 <= v < NT:
                    hd, t = v // KT, v % KT
                    pe.wait_ge(*low_part(v))
                    if t == 0 and hd >= 1:
                        pe.wait_ge(q["o_raw_ok"], hd)
                    last = mm3(banks[2][0:HK, :], VH[:, hd, t, 0:HK], VL[:, hd, t, 0:HK],
                               PH[v % 4][:], PL[v % 4][:], t == 0, t == KT - 1)
                    last.then_inc(q["pv_ok"], 1)
                    if t == KT - 1:
                        pe.wait_ge(q["pv_ok"], v + 1)
                        pe.sem_inc(q["head_done"], 1)
                if s - LAG - KT >= 0 and (s - LAG - KT) % KT == G + 2:
                    project_out((s - LAG - KT) // KT)
            hd = KV - 1
            for g in range(G):
                if g == 0:
                    for pair in range(2):
                        pe.wait_ge(aux_free[pair], sum(1 for i in range(len(aux_items)) if i % 2 == pair))
                pe.wait_ge(q["recip_ok"], G * hd + g + 1)
                pe.matmul(banks[4 + g][0:HD, 0:T], ones_row[HD:HK, :], o_raw[HD:HK, g * T:(g + 1) * T],
                          start=True, stop=True).then_inc(q["bc_last"], 1)
                if g >= 1:
                    project_head(hd, g - 1)
            project_head(hd, G - 1)

            def transposes(k, done):
                pe.wait_ge(q["xn_ok"], k + 1)
                for k4 in range(KD):
                    last = pe.transpose(banks[4][:, k4 * T:(k4 + 1) * T], x_n[:, k4 * P:(k4 + 1) * P], ident[:])
                last.then_inc(q[done], 1)

            transposes(1, "x2T_tr")
            pe.wait_ge(q["x2T_ok"], 1)
            for part, (w_in, s_in, done) in enumerate(((w_inu, "winu_in", "u_filled"), (w_ing, "wing_in", "g_filled"))):
                pe.wait_ge(q[s_in], 16)
                for i in range(DT):
                    for k4 in range(KD):
                        last = pe.matmul(banks[2 * part + i // 4][:, (i % 4) * T:(i % 4 + 1) * T],
                                         w_in[:, k4, i * P:(i + 1) * P], x_T[:, k4, :],
                                         start=(k4 == 0), stop=(k4 == KD - 1))
                    if i % 4 == 3:
                        last.then_inc(q[done], 1)
            pe.wait_ge(q["wx_in"], 48)
            for i in range(DT):
                pe.wait_ge(q["u_ok"], i // 4 + 1)
                last = pe.matmul(banks[4][:, 0:R + 2 * N], u_c[:, i, :], w_x[:, i, :], start=(i == 0), stop=(i == DT - 1))
            last.then_inc(q["ssm_filled"], 1)
            pe.wait_ge(q["spn_ok"], 3)
            pe.transpose(banks[5][0:R + 2 * N, 0:T], sp[:], ident[:]).then_inc(q["tr_filled"], 1)
            pe.wait_ge(q["dtbc_ok"], 4)
            for i in range(DT):
                last = pe.matmul(banks[6 + i // 4][:, (i % 4) * T:(i % 4 + 1) * T], w_dt[:, i * P:(i + 1) * P],
                                 dt_t[:], start=True, stop=True)
                if i % 4 == 3:
                    last.then_inc(q["delta_filled"], 1)
            for k in range(8):
                if k >= 4:
                    pe.wait_ge(*((q["bb_act"], k - 3) if k < 6 else (q["bb_dve"], k - 5)))
                if k == 0:
                    pe.wait_ge(q["bc_low"], 1)
                    pe.wait_ge(q["ident_ok"], 1)
                for m in range(4):
                    row = R + 4 * k + m
                    pick = ident_r[R:R + 2 * N, row:row + 1].to_broadcast([2 * N, P])
                    dst = banks[(0, 1, 4, 5)[k % 4]][:, m * T:(m + 1) * T]
                    pe.matmul(dst, pick, bc_h[R:R + 2 * N, :], start=True, stop=False)
                    last = pe.matmul(dst, pick, bc_l[R:R + 2 * N, :], start=False, stop=True)
                last.then_inc(q["bb_filled"], 1)

            def mamba_out(i):
                pe.wait_ge(q["y2_ok"], i + 1)
                if i == 0:
                    pe.wait_ge(q["gs_ok"], 2)
                    pe.wait_ge(q["wout_in"], 16)
                last = pe.matmul(banks[2][:, :], y2[i % 2][:], w_out[:, i, :], start=(i == 0), stop=(i == DT - 1))
                last.then_inc(q["y2_used"], 1)

            pe.wait_ge(q["delta_ok"], 2)
            for i in range(DT):
                pe.wait_ge(q["yc_ok"], i + 1)
                if i >= 2:
                    pe.wait_ge(q["y1_ok"], i - 1)
                for m in range(N):
                    last = pe.matmul(banks[6 + i % 2][:, 0:T], ident[:], dBu[i % 3][:, m, :],
                                     start=(m == 0), stop=(m == N - 1))
                last.then_inc(q["y_filled"], 1)
                if i >= 1:
                    mamba_out(i - 1)
            mamba_out(DT - 1)
            pe.wait_ge(q["y2_used"], DT)
            pe.sem_inc(q["mo_filled"], 1)
            def down(m):
                pe.wait_ge(q["h_part"], m + 1)
                if m == 0:
                    pe.wait_ge(*scaled(len(units) - 1))
                for i in range(GI * m, min(GI * m + GI, IT)):
                    w = w_dn[:, i, :] if i < IT - 1 else w_dnx[:, 0, :]
                    last = pe.matmul(banks[5][:, :], h_T[:, i, :], w, start=(i == 0), stop=(i == IT - 1))
                if m == ffn_groups() - 1:
                    last.then_inc(q["down_filled"], 1)

            transposes(2, "x3T_tr")
            pe.wait_ge(q["x3T_ok"], 1)
            pe.wait_ge(*scaled(max(i for i, u in enumerate(units) if u[0] != "down")))
            for m in range(ffn_groups()):
                if m >= 2:
                    pe.wait_ge(q["h_part"], m - 1)
                for side, w in enumerate((w_gate, w_up)):
                    for c in range(min(GI, IT - GI * m)):
                        i = GI * m + c
                        for k4 in range(KD):
                            last = pe.matmul(banks[2 * (m % 2) + side][:, c * T:(c + 1) * T],
                                             w[:, k4, i * P:(i + 1) * P], x_T[:, k4, :],
                                             start=(k4 == 0), stop=(k4 == KD - 1))
                last.then_inc(q["gu_filled"], 1)
                if m >= 1:
                    down(m - 1)
            down(ffn_groups() - 1)


def ffn_groups():
    return (IT + GI - 1) // GI


def kv_parts(j):
    return 3 if j == 0 else 2 + CH // P


def key_moves(dst, src, part, lo, hi):
    w = hi - lo
    if part == 0:
        moves = [(dst[0:HD, 0:2, lo:hi], src[0:HD, 0:2 * w].rearrange("p (h t) -> p h t", h=2))]
    else:
        moves = [(dst[0:HD, 2, lo:hi], src[0:HD, 0:w])]
    third = HD // (KV - 1)
    for m in range(2 - part):
        tile = 2 * part + m
        moves.append((dst[tile * third:(tile + 1) * third, KV - 1, lo:hi], src[HD:P, m * w:(m + 1) * w]))
    return moves


def kv_items_upto(j):
    return sum(kv_parts(i) for i in range(j + 1))


def down_tiles(h):
    lo = (h * KT * VW) // D
    hi = ((h + 1) * KT * VW) // D
    return lo, (IT if h == KV - 1 else hi)


def units_of(h):
    u = [(k, h, c) for k in ("gate", "up") for c in range(I // ZC)]
    lo, hi = down_tiles(h)
    return u + [("down", i, 0) for i in range(lo, hi)]


def kernel(**inputs):
    import numpy as np
    import concourse.bacc as bacc
    from concourse.bass_utils import run_bass_kernel_spmd

    def rows(a, parts=P):
        return np.ascontiguousarray(a.reshape(-1, parts, a.shape[-1]).transpose(1, 0, 2))

    v = {k: np.asarray(a) for k, a in inputs.items()}
    m = {k[8:] if k.startswith("L0_attn_") else k: a for k, a in v.items()}
    third = HD // (KV - 1)
    k_rows = [r for h in range(KV - 1) for r in (*range(h * HD, (h + 1) * HD),
                                                 *range((KV - 1) * HD + h * third, (KV - 1) * HD + (h + 1) * third))]
    data = {
        "x": v["x"][0],
        "ctx": rows(v["ctx_4096"][0].T),
        "wq": rows(v["L0_xattn_Wq"].T),
        "wk": rows(v["L0_xattn_Wk"][k_rows].T),
        "wv": rows(v["L0_xattn_Wv"].T),
        "wo": rows(v["L0_xattn_Wo"].T, HD),
        "w_in": rows(m["W_in"].T),
        "conv_w": rows(m["conv_w"]),
        "conv_b": m["conv_b"].reshape(DT, P).T,
        "a": rows(m["A"]),
        "d": m["D_param"].reshape(DT, P).T,
        "ln_dt": m["dt_ln_w"].reshape(R, 1),
        "ln_b": m["b_ln_w"].reshape(N, 1),
        "ln_c": m["c_ln_w"].reshape(N, 1),
        "w_x": rows(m["Wx"].T),
        "w_dt": m["Wdt"].T,
        "dt_bias": m["dt_bias"].reshape(1, DI),
        "w_out": rows(m["W_out"].T),
        "gate_w": rows(v["L0_ffn_gate_w"]),
        "up_w": rows(v["L0_ffn_up_w"]),
        "down_w": rows(v["L0_ffn_down_w"]),
        "gate_z": v["L0_ffn_gate_z"], "gate_s": v["L0_ffn_gate_s"],
        "up_z": v["L0_ffn_up_z"], "up_s": v["L0_ffn_up_s"],
        "down_z": v["L0_ffn_down_z"], "down_s": v["L0_ffn_down_s"],
    }
    nc = bacc.Bacc("TRN2", target_bir_lowering=False, num_devices=1)
    arrays, aps = {}, {}
    for name, a in data.items():
        a = np.ascontiguousarray(a)
        arrays["in_" + name] = a
        aps[name] = nc.dram_tensor("in_" + name, a.shape, mybir.dt.from_np(a.dtype), kind="ExternalInput").ap()
    out = nc.dram_tensor("y", (T, D), F32, kind="ExternalOutput").ap()
    build(nc, aps, out)
    r = run_bass_kernel_spmd(nc, [arrays], core_ids=[0])
    return r.results[0]["y"].reshape(1, T, D)
```

```python
from contextlib import ExitStack

import concourse.bass as bass
from concourse import mybir

F32 = mybir.dt.float32
F32R = mybir.dt.float32r
I32 = mybir.dt.int32
ALU = mybir.AluOpType
ACT = mybir.ActivationFunctionType
AX_X = mybir.AxisListType.X

P = 128
T = 128
D = 512
KD = D // P
CTX = 2048
S = CTX + T
KV, G, HD = 4, 4, 96
HK = HD + 1
VW = HD + 2
CH = 256
NCH = 1 + CTX // CH
KT = S // P
NT = KV * KT
LAG = 4
NP = LAG + 1
DI = 1024
DT = DI // P
N = 16
R = 32
TAPS = 4
I = 1792
IT = I // P
GI = 4
ZC = 448
DVE_STEPS = ((2, 5, 8, 11, 14), (2, 5, 8, 11, 14), (2, 5, 8, 11, 14), (1, 3, 5, 7, 9, 11, 13, 15))
SPLIT = (IT - 1) // GI * GI
EARLY = 6
LATE = 7
DT_B_C = ((0, R), (R, R + N), (R + N, R + 2 * N))
SCALE = float(HD) ** -0.5
LN_EPS = 1e-5
RMS_EPS = 1e-6


def chunk_cols(j):
    return (CTX, CTX + T) if j == 0 else ((j - 1) * CH, j * CH)


def build(nc, A, out):
    with ExitStack() as ctx:
        count = [0]

        def sem(name):
            return ctx.enter_context(nc.semaphore(name))

        def bank(name):
            return ctx.enter_context(nc.psum_tensor(name, [P, 512], F32))

        def at(offset, name, shape, dt=F32):
            with ExitStack() as hold:
                if offset:
                    count[0] += 1
                    hold.enter_context(nc.sbuf_tensor(f"skip{count[0]}", [P, offset // 4], F32))
                return hold.enter_context(nc.sbuf_tensor(name, shape, dt))

        class Row:
            def __init__(self, start):
                self.at = start

            def put(self, name, shape, dt=F32):
                n = 4
                for s in shape[1:]:
                    n *= s
                t = at(self.at, name, shape, dt)
                self.at += (n + 31) // 32 * 32
                return t

        fixed = Row(0)
        x_res = fixed.put("x_res", [P, D])
        x_n = fixed.put("x_n", [P, D])
        ident = fixed.put("ident", [P, P])
        conv_w = fixed.put("conv_w", [P, DT, TAPS])
        conv_b = fixed.put("conv_b", [P, DT])
        a_par = fixed.put("a_par", [P, DT, N])
        d_par = fixed.put("d_par", [P, DT])
        ln_b = fixed.put("ln_b", [P, R + 2 * N])
        stats = fixed.put("stats", [P, 8])
        norm = fixed.put("norm", [P, 8])
        eps = fixed.put("eps", [P, 2])
        neg_max = fixed.put("neg_max", [P, HD + KV * G], F32R)
        part_max = fixed.put("part_max", [P, G, NCH])
        one = fixed.put("one", [P, 1])
        r_sum = fixed.put("r_sum", [P, G])
        ident_r = fixed.put("ident_r", [P, P], F32R)
        zs = fixed.at
        x_nT = at(zs, "x_nT", [P, KD, T])
        k_at = zs + 2 * D * 4

        keys = Row(k_at)
        KH = keys.put("KH", [HK, KV, S], F32R)
        kl_at = keys.at
        KL = keys.put("KL", [HK, KV, S], F32R)
        vh_at = keys.at
        VH = keys.put("VH", [P, KV, KT, VW], F32R)
        vl_at = keys.at
        VL = keys.put("VL", [P, KV, KT, VW], F32R)
        q_at = keys.at
        QH = keys.put("QH", [HK, KV, G * T], F32R)
        QL = keys.put("QL", [HK, KV, G * T], F32R)
        r_at = keys.at
        proj = Row(r_at)
        WKH, WKL, WVH, WVL = [proj.put(n, [P, KD, KV * HD], F32R) for n in ("WKH", "WKL", "WVH", "WVL")]
        HH = [proj.put(f"HH{i}", [P, KD, CH], F32R) for i in range(2)]
        HL = [proj.put(f"HL{i}", [P, KD, CH], F32R) for i in range(2)]
        c_raw = [proj.put(f"c_raw{i}", [P, KD, CH]) for i in range(2)]
        w_raw = [proj.put(f"w_raw{i}", [P, KD, KV * HD]) for i in range(2)]

        att = Row(r_at)
        PR = [att.put(f"PR{i}", [P, G * T]) for i in range(3)]
        PH = [att.put(f"PH{i}", [P, G * T], F32R) for i in range(NP)]
        PL = [att.put(f"PL{i}", [P, G * T], F32R) for i in range(NP)]
        WO = [att.put(f"WO{i}", [HD, G, D]) for i in range(2)]
        w_out_at = att.at
        w_out = att.put("w_out", [P, DT, D])
        o_raw_at = att.at
        o_raw = att.put("o_raw", [HK, G * T])

        ZB = D * 4
        z_b = [at(o, f"z_b{i}", [P, D], I32) for i, o in enumerate((q_at, q_at + 4 * ZB, vl_at, q_at + 5 * ZB, o_raw_at))]
        s_b = [at(o, f"s_b{i}", [P, D]) for i, o in enumerate((zs, zs + ZB, vl_at + ZB, vl_at, vl_at + 12 * ZB))]

        w_gate = at(k_at, "w_gate", [P, KD, I])
        w_up = at(kl_at, "w_up", [P, KD, I])
        tail = KD * I * 4
        w_x = at(k_at + tail, "w_x", [P, DT, R + 2 * N])
        w_dt = at(k_at + tail + DT * (R + 2 * N) * 4, "w_dt", [R + 1, DI])
        w_dn = at(vh_at, "w_dn", [P, IT - 1, D])
        w_dnx = at(kl_at + tail, "w_dnx", [P, 1, D])
        w_inu = at(vl_at + ZB, "w_inu", [P, KD, DI])
        w_ing = at(r_at, "w_ing", [P, KD, DI])

        ROW, STATES, ROWS = D * 4, N * T * 4, DT * T * 4
        mam = Row(r_at + ROW)
        B_b = mam.put("B_b", [P, N, T])
        C_b = mam.put("C_b", [P, N, T])
        dA_at = mam.at
        dA = [mam.put(f"dA{i}", [P, N, T]) for i in range(2)]
        u_c = mam.put("u_c", [P, DT, T])
        assert mam.at <= w_out_at
        delta = at(q_at + 2 * ROW, "delta", [P, DT, T])
        sig = at(dA_at + STATES, "sig", [P, DT, T])
        d_diag = at(kl_at + tail + D * 4, "d_diag", [P, DT, P])
        dBu = [at(o, f"dBu{i}", [P, N, T]) for i, o in enumerate((vl_at, vl_at + STATES, q_at + 5 * ROW))]
        du = at(vl_at + 2 * STATES, "du", [P, DT, T])
        g_s = at(vl_at + 2 * STATES + ROWS, "g_s", [P, DT, T])
        x_T = x_n[:, :].rearrange("p (k t) -> p k t", k=KD)
        small = Row(q_at + ROW)
        sp = small.put("sp", [P, R + 2 * N])
        sq = small.put("sq", [P, R + 2 * N])
        dt_t = small.put("dt_t", [R + 1, T])
        sp_h = small.put("sp_h", [P, 2 * N], F32R)
        sp_l = small.put("sp_l", [P, 2 * N], F32R)
        y2 = [at(q_at + ROW + T * 4 * i, f"y2{i}", [P, T]) for i in range(2)]

        ffn = Row(r_at)
        f_sig = [ffn.put(f"f_sig{i}", [P, GI * T]) for i in range(2)]
        h_T = ffn.put("h_T", [P, IT, T])
        y_out = ffn.put("y_out", [P, D])
        w_dnH = ffn.put("w_dnH", [P, SPLIT, D], F32R)
        w_dnL = at(vh_at, "w_dnL", [P, SPLIT, D], F32R)
        h_H, h_L = [ffn.put(f"h_{c}", [P, SPLIT, T], F32R) for c in "HL"]

        banks = [bank(f"bank{i}") for i in range(8)]
        aux = [[banks[4], banks[5]], [banks[6], banks[7]]]

        names = (
            "x_in wk_in wv_in wo_in0 wo_in1 wout_in winu_in wing_in wx_in par_in ctx_in0 ctx_in1 wq_in0 wq_in1 "
            "z_in0 z_in1 z_in2 wgate_in wup_in wdn_in out_done "
            "consts pads stat_ok rstd_ok xn_ok wk_split wv_split ctx_split wraw_free wq_free raw_free "
            "kv_filled kv_high kv_free aux_filled0 aux_filled1 aux_free0 aux_free1 q_high xT_copy xT_high wk_high tail_low "
            "proj_done max_ok s_filled exp_ok pl_pool pl_dve pv_ok head_done o_raw_ok sums_filled recip_ok x_acc ident_ok "
            "deq_sub deq_pool deq_dve nT_filled nT_act nT_dve u_filled g_filled conv_a conv_ok sil_a u_ok gsil_a gs_ok "
            "ssm_filled rms_ok spn_ok bc_split tr_filled dt_ok dt_one diag_ok delta_filled neg_ok nabs_ok dl_a delta_ok du_ok "
            "bb_filled bb_act bb_dve zero_ok dA_ok dBu_dve dBu_pool scan_ok yc_ok yc_pool y_filled y2_ok y2_used "
            "gu_filled fs_a wdn_high wdn_low h_part h_high h_low down_filled fin_ok act_seq dve_seq"
        ).split()
        q = {n: sem(n) for n in names}
        aux_filled = [q["aux_filled0"], q["aux_filled1"]]
        aux_free = [q["aux_free0"], q["aux_free1"]]

        aux_items = []
        step_extra = {}

        def add_aux(item):
            aux_items.append(item)

        pre = {}
        pre[0] = [("q", 0)]
        for j in range(1, NCH):
            pre[j] = [("mx", 0, j - 1)]
            if j in (1, 4):
                pre[j].append(("q", (j + 2) // 3))
        between = {NCH - 1: pre[NCH - 1]}
        pre[NCH - 1] = [("mx", 0, NCH - 1), ("q", KV - 1), ("nm", 0), ("mx", 1, 0)]
        for step in range(NT + LAG):
            todo = []
            h, t = step // KT, step % KT
            if h + 1 < KV:
                todo += [("mx", h + 1, j) for j in range(int(h == 0), NCH) if t == 3 * j // 2]
                if t == 15:
                    todo.append(("nm", h + 1))
            if h >= 1 and t in (LAG + 2, LAG + 5):
                todo.append(("pr", h - 1, int(t == LAG + 5)))
            step_extra[step] = todo
        add_aux(("xT",))
        for j in range(NCH):
            for it in between.get(j, []) + pre[j]:
                add_aux(it)
        for step in range(NT + LAG):
            for it in step_extra[step]:
                add_aux(it)
        for half in range(2):
            add_aux(("pr", KV - 1, half))
        aux_index = {it: i for i, it in enumerate(aux_items)}

        def aux_of(item):
            i = aux_index[item]
            return i % 2, i // 2

        def projected(h):
            pair, k = aux_of(("pr", h, 1))
            return aux_filled[pair], k + 1

        def piece(kind, g, c):
            if kind == "down":
                return w_dn[:, g, :] if g < IT - 1 else w_dnx[:, 0, :]
            return (w_gate if kind == "gate" else w_up)[:, g, c * ZC:(c + 1) * ZC]

        units = [u for h in range(KV) for u in units_of(h)]
        owner = [h for h in range(KV) for _ in units_of(h)]

        def zeros_at(u):
            return z_b[u % 3 if u % 3 < 2 else (2, 3, 3, 4)[owner[u]]]

        def scales_at(u):
            return s_b[u % 3 if u % 3 < 2 else (2, 3, 3, 4)[owner[u]]]

        def scaled_by_dve(u):
            kind, _, c = units[u]
            return kind == "down" or (owner[u] == KV - 2 and c % 2 == 1)

        def scaled(u):
            n = sum(scaled_by_dve(i) for i in range(u + 1))
            return (q["deq_dve"], n) if scaled_by_dve(u) else (q["deq_pool"], u + 1 - n)

        def deq_at(s):
            h, t = s // KT, s % KT
            return int(1 <= h < KV and 6 <= t < (KT if h < KV - 1 else 14))

        def on_dve(s):
            h, t = s // KT, s % KT
            return t in DVE_STEPS[h]

        def low_part(s):
            n = sum(on_dve(i) for i in range(s + 1))
            return (q["pl_dve"], n) if on_dve(s) else (q["pl_pool"], s + 1 - n)

        def u_bank(i):
            return banks[(0, 1, 6, 7)[i // 2]]

        def bcast(k):
            return ((B_b if k < 4 else C_b)[:, 4 * (k % 4):4 * (k % 4) + 4, :],
                    banks[(0, 1, 4, 5)[k % 4]][:, :].rearrange("p (i t) -> p i t", i=4))

        def parts_before(i):
            return i + (i > 0)

        block = ctx.enter_context(nc.Block())

        @block.sync
        def _(sp_q):
            def load(dst, src, s):
                sp_q.dma_start(dst, src).then_inc(q[s], 16)

            load(x_res[:], A["x"], "x_in")
            load(w_raw[0][:], A["wk"], "wk_in")
            load(c_raw[0][:], A["ctx"][:, :, 0:CH], "ctx_in0")
            load(w_raw[1][:], A["wv"], "wv_in")
            load(c_raw[1][:], A["ctx"][:, :, CH:2 * CH], "ctx_in1")
            nq = 0
            for j in range(1, NCH):
                if nq < KV:
                    if nq < 2:
                        sp_q.wait_ge(q["wraw_free"], nq + 1)
                    else:
                        sp_q.wait_ge(q["wq_free"], nq - 1)
                    load(w_raw[nq % 2][:], A["wq"][:, :, nq * G * HD:(nq + 1) * G * HD], f"wq_in{nq % 2}")
                    nq += 1
                if j + 2 < NCH:
                    sp_q.wait_ge(q["raw_free"], j)
                    load(c_raw[(j + 1) % 2][:], A["ctx"][:, :, (j + 1) * CH:(j + 2) * CH], f"ctx_in{(j + 1) % 2}")
            load(conv_w[:], A["conv_w"], "par_in")
            load(conv_b[:], A["conv_b"], "par_in")
            load(a_par[:], A["a"], "par_in")
            load(d_par[:], A["d"], "par_in")
            load(ln_b[:, 0:R], A["ln_dt"].to_broadcast([P, R]), "par_in")
            load(ln_b[:, R:R + N], A["ln_b"].to_broadcast([P, N]), "par_in")
            load(ln_b[:, R + N:R + 2 * N], A["ln_c"].to_broadcast([P, N]), "par_in")
            sp_q.wait_ge(q["proj_done"], 1)
            load(WO[0][:], A["wo"][:, 0:G, :], "wo_in0")
            load(WO[1][:], A["wo"][:, G:2 * G, :], "wo_in1")
            load(w_out[:], A["w_out"], "wout_in")
            unit = 0

            def load_unit():
                nonlocal unit
                if unit >= 3:
                    sp_q.wait_ge(*scaled(unit - 3))
                if zeros_at(unit) is z_b[4]:
                    sp_q.wait_ge(*projected(KV - 1))
                kind, g, c = units[unit]
                n = D if kind == "down" else ZC
                for dst, src in ((zeros_at(unit), A[kind + "_z"]), (scales_at(unit), A[kind + "_s"])):
                    load(dst[:, 0:n], src[g:g + 1, c * n:(c + 1) * n].to_broadcast([P, n]), f"z_in{unit % 3}")
                unit += 1

            for h in range(KV):
                sp_q.wait_ge(q["head_done"], h + 1)
                if h == KV - 1:
                    load(w_ing[:], A["w_in"][:, :, DI:2 * DI], "wing_in")
                    load(w_x[:], A["w_x"], "wx_in")
                    load(w_dt[0:R, :], A["w_dt"], "wx_in")
                    load(w_dt[R:R + 1, :], A["dt_bias"], "wx_in")
                load(w_gate[:, h, :].bitcast(I32), A["gate_w"][:, h, :], "wgate_in")
                for _ in range(3):
                    load_unit()
                load(w_up[:, h, :].bitcast(I32), A["up_w"][:, h, :], "wup_in")
                lo, hi = down_tiles(h)
                load(w_dn[:, lo:min(hi, IT - 1), :].bitcast(I32), A["down_w"][:, lo:min(hi, IT - 1), :], "wdn_in")
                if hi == IT:
                    load(w_dnx[:].bitcast(I32), A["down_w"][:, IT - 1:IT, :], "wdn_in")
                while unit < len(units) and owner[unit] == h:
                    load_unit()
                if h == KV - 2:
                    load(w_inu[:], A["w_in"][:, :, 0:DI], "winu_in")
                if h + 2 < KV:
                    sp_q.wait_ge(*projected(h))
                    load(WO[h % 2][:], A["wo"][:, (h + 2) * G:(h + 3) * G, :], f"wo_in{h % 2}")
            sp_q.wait_ge(q["fin_ok"], 1)
            sp_q.dma_start(out, y_out[:]).then_inc(q["out_done"], 16)
            sp_q.wait_ge(q["out_done"], 16)

        @block.gpsimd
        def _(pool):
            pool.memset(ident[:], 0.0).then_inc(q["zero_ok"], 1)
            pool.memset(eps[:, 0:1], LN_EPS)
            pool.memset(eps[:, 1:2], RMS_EPS)
            pool.memset(neg_max[:].bitcast(F32), 0.0)
            pool.memset(one[:], 1.0)
            pool.wait_ge(q["zero_ok"], 1)
            pool.affine_select(out=ident[:], in_=ident[:], compare_op=ALU.not_equal, fill=1.0, base=0,
                               pattern=[[-1, P]], channel_multiplier=1).then_inc(q["consts"], 1)
            for j in range(1, NCH):
                b = (j - 1) % 2
                pool.wait_ge(q[f"ctx_in{b}"], 16 * ((j - 1) // 2 + 1))
                if j >= 2:
                    pool.wait_ge(q["kv_filled"], kv_items_upto(j - 2))
                pool.tensor_scalar(HH[j % 2][:], c_raw[b][:], 1.0, None, ALU.mult).then_inc(q["ctx_split"], 1)
                pool.wait_ge(q["ctx_split"], 2 * j - 1)
                pool.tensor_tensor(HL[j % 2][:], c_raw[b][:], HH[j % 2][:].bitcast(F32),
                                   ALU.subtract).then_inc(q["ctx_split"], 1)
                pool.wait_ge(q["ctx_split"], 2 * j)
                pool.sem_inc(q["raw_free"], 1)
                if j == 1:
                    for m, (cells, value) in enumerate(((KH[HD:HK, :, :], 1.0), (KL[HD:HK, :, :], 0.0),
                                                        (QL[HD:HK, :, :], 0.0), (VH[:, :, :, HD:VW], 1.0),
                                                        (VL[:, :, :, HD:VW], 0.0))):
                        pool.memset(cells.bitcast(F32), value).then_inc(q["pads"], 1)
                        pool.wait_ge(q["pads"], m + 1)
            unit = 0

            def scale_unit():
                nonlocal unit
                kind, g, c = units[unit]
                if not scaled_by_dve(unit):
                    pool.wait_ge(q["deq_sub"], unit + 1)
                    w = piece(kind, g, c)
                    pool.tensor_tensor(w, w, scales_at(unit)[:, 0:ZC], ALU.mult).then_inc(q["deq_pool"], 1)
                unit += 1

            for s in range(NT):
                if not on_dve(s):
                    pool.wait_ge(q["exp_ok"], s + 1)
                    if s >= NP:
                        pool.wait_ge(q["pv_ok"], s - LAG)
                    pool.tensor_tensor(PL[s % NP][:], PR[s % 3][:], PH[s % NP][:].bitcast(F32),
                                       ALU.subtract).then_inc(q["pl_pool"], 1)
                for _ in range(deq_at(s)):
                    scale_unit()
            pool.wait_ge(q["head_done"], KV)
            pool.memset(dA[0][:, :, 0:1], 0.0).then_inc(q["zero_ok"], 1)
            while unit < len(units) - LATE:
                scale_unit()
            pool.wait_ge(q["delta_ok"], 2)
            pool.memset(dA[1][:, :, 0:1], 0.0).then_inc(q["zero_ok"], 1)
            pool.wait_ge(q["bb_act"], 1)
            pool.wait_ge(q["bb_dve"], 3)
            pool.wait_ge(q["du_ok"], 1)
            for i in range(1, DT):
                if i >= 3:
                    pool.wait_ge(q["y_filled"], i - 2)
                pool.tensor_tensor(dBu[i % 3][:], B_b[:], du[:, i:i + 1, :].to_broadcast([P, N, T]),
                                   ALU.mult).then_inc(q["dBu_pool"], 1)
            pool.wait_ge(q["scan_ok"], parts_before(DT - 1))
            half = slice(N // 2, N)
            pool.tensor_tensor(dBu[(DT - 2) % 3][:, half, :], dBu[(DT - 2) % 3][:, half, :], C_b[:, half, :],
                               ALU.mult).then_inc(q["yc_pool"], 1)

            def down_low(i):
                pool.wait_ge(q["wdn_high"], i + 1)
                pool.tensor_tensor(w_dnL[:, i, :], w_dn[:, i, :], w_dnH[:, i, :].bitcast(F32),
                                   ALU.subtract).then_inc(q["wdn_low"], 1)

            for i in range(EARLY):
                down_low(i)
            while unit < len(units):
                scale_unit()
            for i in range(EARLY, SPLIT):
                down_low(i)

        @block.scalar
        def _(act):
            def rstd(src, dst, e, scale=1.0):
                act.activation(dst, src, ACT.Ln, bias=e, scale=scale).then_inc(q["act_seq"], 1)
                seq[0] += 1
                act.wait_ge(q["act_seq"], seq[0])
                return act.activation(dst, dst, ACT.Exp, scale=-0.5)

            seq = [0]

            def chain(ins):
                ins.then_inc(q["act_seq"], 1)
                seq[0] += 1
                act.wait_ge(q["act_seq"], seq[0])

            def take_nT(k):
                act.wait_ge(q["nT_filled"], 2 * k)
                act.activation(x_T[:, 0:KD // 2, :], banks[4][:, 0:2 * T].rearrange("p (k t) -> p k t", k=2),
                               ACT.Copy).then_inc(q["nT_act"], 1)

            act.preload_act_table_set("natural_log_exp_and_others")
            act.wait_ge(q["consts"], 1)
            act.wait_ge(q["stat_ok"], 1)
            rstd(stats[:, 7:8], norm[:, 0:1], eps[:, 0:1]).then_inc(q["rstd_ok"], 1)

            def evac_aux(item):
                pair, k = aux_of(item)
                act.wait_ge(aux_filled[pair], k + 1)
                src = aux[pair][0]
                if item[0] == "xT":
                    v = src[:, :].rearrange("p (k t) -> p k t", k=KD)
                    act.activation(HH[0][:, :, 0:T], v, ACT.Copy).then_inc(q["xT_high"], 1)
                    act.wait_ge(q["tail_low"], 1)
                    act.activation(x_nT[:], v, ACT.Copy).then_inc(q["xT_copy"], 1)
                elif item[0] == "q":
                    act.activation(QH[0:HD, item[1], :], src[0:HD, :], ACT.Copy).then_inc(q["q_high"], 1)
                elif item[0] == "nm":
                    act.activation(QH[HD:HK, item[1], :], src[HD:HK, :], ACT.Copy).then_inc(aux_free[pair], 1)

            act.wait_ge(q["wk_in"], 16)
            for half in range(2):
                k = slice(KD // 2 * half, KD // 2 * (half + 1))
                act.activation(WKH[:, k, :], w_raw[0][:, k, :], ACT.Copy).then_inc(q["wk_high"], 1)
            evac_aux(("xT",))
            n = 0
            for j in range(NCH):
                lo, hi = chunk_cols(j)
                for part in range(kv_parts(j)):
                    act.wait_ge(q["kv_filled"], n + 1)
                    src = banks[n % 4]
                    if part < 2:
                        for dst, v in key_moves(KH, src, part, lo, hi):
                            last = act.activation(dst, v, ACT.Copy)
                        last.then_inc(q["kv_high"], 1)
                    else:
                        v = src[:, 0:KV * HD].rearrange("p (h d) -> p h d", h=KV)
                        act.activation(VH[:, :, lo // P + part - 2, 0:HD], v, ACT.Copy).then_inc(q["kv_high"], 1)
                    n += 1
                for item in pre[j]:
                    if item[0] in ("q", "nm"):
                        evac_aux(item)

            for s in range(NT + LAG):
                h, t = s // KT, s % KT
                if s < NT:
                    act.wait_ge(q["s_filled"], s + 1)
                    if s >= 3:
                        act.wait_ge(*low_part(s - 3))
                    elif s == 0:
                        act.wait_ge(q["proj_done"], 1)
                    if s >= NP:
                        act.wait_ge(q["pv_ok"], s - LAG)
                    act.activation(PH[s % NP][:], banks[s % 2][:, :], ACT.Exp, scale=SCALE)
                    act.activation(PR[s % 3][:], banks[s % 2][:, :], ACT.Exp, scale=SCALE).then_inc(q["exp_ok"], 1)
                if s >= LAG and (s - LAG) % KT == KT - 1:
                    hd = (s - LAG) // KT
                    act.wait_ge(q["head_done"], hd + 1)
                    if hd >= 1:
                        act.wait_ge(*projected(hd - 1))
                    act.activation(o_raw[:], banks[2][0:HK, :], ACT.Copy).then_inc(q["o_raw_ok"], 1)
                for item in step_extra[s]:
                    if item[0] == "nm":
                        evac_aux(item)

            act.wait_ge(q["par_in"], 16 * 7)
            for i in range(DT):
                last = act.activation(d_diag[:, i, :], ident[:], ACT.Copy, scale=d_par[:, i:i + 1])
            last.then_inc(q["diag_ok"], 1)
            act.wait_ge(q["stat_ok"], 2)
            rstd(stats[:, 7:8], norm[:, 0:1], eps[:, 0:1]).then_inc(q["rstd_ok"], 1)
            take_nT(1)

            def sigmoid(dst, src):
                chain(act.activation(dst, src, ACT.Exp, scale=-1.0))
                chain(act.activation(dst, dst, ACT.Ln, bias=1.0))
                return act.activation(dst, dst, ACT.Exp, scale=-1.0)

            for p in range(DT // 2 + 1):
                if p < DT // 2:
                    act.wait_ge(q["u_filled"], p + 1)
                    for i in (2 * p, 2 * p + 1):
                        last = act.activation(u_c[:, i, :], u_bank(i)[:, (i % 2) * T:(i % 2 + 1) * T], ACT.Identity,
                                              bias=conv_b[:, i:i + 1], scale=conv_w[:, i, TAPS - 1:TAPS])
                    last.then_inc(q["conv_a"], 1)
                if p >= 1:
                    sl = slice(2 * p - 2, 2 * p)
                    act.wait_ge(q["conv_ok"], 2 * p)
                    sigmoid(sig[:, sl, :], u_c[:, sl, :]).then_inc(q["sil_a"], 1)

            def gate_sigmoid(half):
                act.wait_ge(q["g_filled"], half + 1)
                sigmoid(g_s[:, 4 * half:4 * half + 4, :],
                        banks[2 + half][:, :].rearrange("p (i t) -> p i t", i=4)).then_inc(q["gsil_a"], 1)

            act.wait_ge(q["ssm_filled"], 1)
            for a, (lo, hi) in enumerate(DT_B_C):
                last = act.activation(sq[:, lo:hi], banks[4][:, lo:hi], ACT.Square, scale=(hi - lo) ** -0.5,
                                      accum_out=norm[:, 2 + a:3 + a])
            chain(last)
            chain(act.activation(norm[:, 2:5], norm[:, 2:5], ACT.Ln, bias=eps[:, 1:2]))
            act.activation(norm[:, 2:5], norm[:, 2:5], ACT.Exp, scale=-0.5).then_inc(q["rms_ok"], 1)
            act.wait_ge(q["tr_filled"], 1)
            act.activation(dt_t[0:R, :], banks[5][0:R, 0:T], ACT.Copy).then_inc(q["dt_ok"], 1)
            gate_sigmoid(0)
            for half in range(2):
                sl = slice(4 * half, 4 * half + 4)
                if half == 0:
                    act.wait_ge(q["delta_filled"], 1)
                    chain(act.activation(sig[:, sl, :], banks[6][:, :].rearrange("p (i t) -> p i t", i=4), ACT.Abs))
                else:
                    act.wait_ge(q["nabs_ok"], 1)
                chain(act.activation(sig[:, sl, :], sig[:, sl, :], ACT.Exp, scale=1.0 if half else -1.0))
                act.activation(sig[:, sl, :], sig[:, sl, :], ACT.Ln, bias=1.0).then_inc(q["dl_a"], 1)
            def take_bcast(k):
                act.wait_ge(q["bb_filled"], k + 1)
                dst, src = bcast(k)
                act.activation(dst, src, ACT.Copy).then_inc(q["bb_act"], 1)

            take_bcast(1)
            for i in range(DT):
                if i < 2:
                    act.wait_ge(q["zero_ok"], 1 + 1 + i)
                    act.wait_ge(q["delta_ok"], 1 + i)
                if i >= 2:
                    act.wait_ge(q["scan_ok"], parts_before(i - 1))
                for m in range(N):
                    last = act.activation(dA[i % 2][:, m, 1:T], delta[:, i, 1:T], ACT.Exp, scale=a_par[:, i, m:m + 1])
                    if (m + 1) % (N // 2) == 0:
                        last.then_inc(q["dA_ok"], 1)
                if i == 1:
                    take_bcast(6)
                    take_bcast(7)
                    gate_sigmoid(1)
            def down_high(i):
                act.wait_ge(*scaled(units.index(("down", i, 0))))
                act.activation(w_dnH[:, i, :], w_dn[:, i, :], ACT.Copy).then_inc(q["wdn_high"], 1)

            dequantised = sum(u[0] == "down" for u in units[:len(units) - LATE])
            act.wait_ge(q["yc_ok"], parts_before(DT - 1) + 2)
            act.wait_ge(q["yc_pool"], 1)
            for i in range(dequantised):
                down_high(i)
            act.wait_ge(q["stat_ok"], 3)
            rstd(stats[:, 7:8], norm[:, 0:1], eps[:, 0:1]).then_inc(q["rstd_ok"], 1)
            take_nT(2)
            for i in range(dequantised, SPLIT):
                down_high(i)
            for m in range(ffn_groups()):
                n = min(GI, IT - GI * m) * T
                act.wait_ge(q["gu_filled"], m + 1)
                if m >= 2:
                    act.wait_ge(q["h_part"], m - 1)
                sigmoid(f_sig[m % 2][:, 0:n], banks[2 * (m % 2)][:, 0:n]).then_inc(q["fs_a"], 1)
                if GI * m < SPLIT:
                    act.wait_ge(q["h_part"], m + 1)
                    g = slice(GI * m, GI * m + GI)
                    act.activation(h_H[:, g, :], h_T[:, g, :], ACT.Copy).then_inc(q["h_high"], 1)

        @block.vector
        def _(dve):
            seq = [0]

            def chain(ins):
                ins.then_inc(q["dve_seq"], 1)
                seq[0] += 1
                dve.wait_ge(q["dve_seq"], seq[0])

            def norm_rows(k):
                chain(dve.bn_stats(stats[:, 0:6], x_res[:]))
                dve.bn_aggr(stats[:, 6:8], stats[:, 0:6]).then_inc(q["stat_ok"], 1)
                dve.wait_ge(q["stat_ok"], k + 1)
                dve.wait_ge(q["rstd_ok"], k + 1)
                for half in range(2):
                    c = slice(half * D // 2, (half + 1) * D // 2)
                    dve.tensor_scalar(x_n[:, c], x_res[:, c], stats[:, 6:7], norm[:, 0:1],
                                      ALU.subtract, ALU.mult).then_inc(q["xn_ok"], 1)

            def take_nT(k):
                dve.wait_ge(q["nT_filled"], 2 * k)
                dve.tensor_copy(x_T[:, KD // 2:, :], banks[5][:, 0:2 * T].rearrange("p (k t) -> p k t",
                                                                                    k=2)).then_inc(q["nT_dve"], 1)

            dve.wait_ge(q["x_in"], 16)
            norm_rows(0)
            dve.wait_ge(q["consts"], 1)
            dve.tensor_copy(ident_r[:], ident[:]).then_inc(q["ident_ok"], 1)
            def wk_low(half):
                k = slice(KD // 2 * half, KD // 2 * (half + 1))
                dve.wait_ge(q["wk_high"], half + 1)
                dve.tensor_tensor(WKL[:, k, :], w_raw[0][:, k, :], WKH[:, k, :].bitcast(F32),
                                  ALU.subtract).then_inc(q["wk_split"], 1)

            wk_low(0)
            pair, k = aux_of(("xT",))
            dve.wait_ge(q["xT_high"], 1)
            dve.tensor_tensor(HL[0][:, :, 0:T], aux[pair][0][:, :].rearrange("p (k t) -> p k t", k=KD),
                              HH[0][:, :, 0:T].bitcast(F32), ALU.subtract).then_inc(q["tail_low"], 1)
            dve.wait_ge(q["tail_low"], 1)
            dve.sem_inc(aux_free[pair], 1)
            wk_low(1)
            dve.wait_ge(q["wk_split"], 2)
            dve.sem_inc(q["wraw_free"], 1)
            dve.wait_ge(q["wv_in"], 16)
            chain(dve.tensor_copy(WVH[:], w_raw[1][:]))
            chain(dve.tensor_tensor(WVL[:], w_raw[1][:], WVH[:].bitcast(F32), ALU.subtract))
            dve.sem_inc(q["wv_split"], 1)
            dve.sem_inc(q["wraw_free"], 1)

            def take_aux(item):
                pair, k = aux_of(item)
                a, b = aux[pair]
                if item == ("pr", item[1], 0):
                    dve.wait_ge(q["sums_filled"], item[1] + 1)
                    dve.reciprocal(r_sum[:], banks[3][:, 0:G]).then_inc(q["recip_ok"], 1)
                    dve.wait_ge(q["recip_ok"], item[1] + 1)
                dve.wait_ge(aux_filled[pair], k + 1)
                if item[0] == "pr":
                    for m, bk in enumerate((a, b)):
                        dve.scalar_tensor_tensor(x_res[:], bk[:, :], r_sum[:, 2 * item[2] + m:2 * item[2] + m + 1],
                                                 x_res[:], ALU.mult, ALU.add).then_inc(q["x_acc"], 1)
                        dve.wait_ge(q["x_acc"], G * item[1] + 2 * item[2] + m + 1)
                    dve.sem_inc(aux_free[pair], 1)
                elif item[0] == "q":
                    h = item[1]
                    dve.wait_ge(q["q_high"], h + 1)
                    dve.tensor_tensor(QL[0:HD, h, :], a[0:HD, :], QH[0:HD, h, :].bitcast(F32),
                                      ALU.subtract).then_inc(aux_free[pair], 1)
                elif item[0] == "mx":
                    _, h, j = item
                    lo, hi = chunk_cols(j)
                    w = hi - lo
                    for m, bk in enumerate((a, b)):
                        last = dve.tensor_reduce(part_max[:, 2 * m:2 * m + 2, j],
                                                 bk[:, 0:2 * w].rearrange("p (g t) -> p g t", g=2), AX_X, ALU.max)
                    last.then_inc(aux_free[pair], 1)
                    if j == NCH - 1:
                        dve.wait_ge(aux_free[pair], k + 1)
                        dve.tensor_reduce(neg_max[:, HD + G * h:HD + G * (h + 1)], part_max[:], AX_X, ALU.max,
                                          negate=True).then_inc(q["max_ok"], 1)
                        dve.wait_ge(q["max_ok"], h + 1)

            unit = 0

            def gate(half):
                sl = slice(4 * half, 4 * half + 4)
                dve.wait_ge(q["gsil_a"], half + 1)
                dve.tensor_tensor(g_s[:, sl, :], g_s[:, sl, :], banks[2 + half][:, :].rearrange("p (i t) -> p i t", i=4),
                                  ALU.mult).then_inc(q["gs_ok"], 1)

            def take_bcast(k):
                dve.wait_ge(q["bb_filled"], k + 1)
                dst, src = bcast(k)
                dve.tensor_copy(dst, src).then_inc(q["bb_dve"], 1)

            def zero_unit():
                nonlocal unit
                kind, g, c = units[unit]
                h = owner[unit]
                loads = h + 1 if (kind, g) != ("down", IT - 1) else KV + 1
                dve.wait_ge(q[{"gate": "wgate_in", "up": "wup_in", "down": "wdn_in"}[kind]], 16 * loads)
                dve.wait_ge(q[f"z_in{unit % 3}"], 32 * (unit // 3 + 1))
                w = piece(kind, g, c)
                n = D if kind == "down" else ZC
                dve.tensor_tensor(w, w.bitcast(I32), zeros_at(unit)[:, 0:n], ALU.subtract).then_inc(q["deq_sub"], 1)
                if scaled_by_dve(unit):
                    dve.wait_ge(q["deq_sub"], unit + 1)
                    dve.tensor_tensor(w, w, scales_at(unit)[:, 0:n], ALU.mult).then_inc(q["deq_dve"], 1)
                unit += 1

            n = 0
            for j in range(NCH):
                lo, hi = chunk_cols(j)
                for part in range(kv_parts(j)):
                    dve.wait_ge(q["kv_high"], n + 1)
                    src = banks[n % 4]
                    if part < 2:
                        for (dst, v), (high, _) in zip(key_moves(KL, src, part, lo, hi), key_moves(KH, src, part, lo, hi)):
                            last = dve.tensor_tensor(dst, v, high.bitcast(F32), ALU.subtract)
                        last.then_inc(q["kv_free"], 1)
                    else:
                        v = src[:, 0:KV * HD].rearrange("p (h d) -> p h d", h=KV)
                        kt = lo // P + part - 2
                        dve.tensor_tensor(VL[:, :, kt, 0:HD], v, VH[:, :, kt, 0:HD].bitcast(F32),
                                          ALU.subtract).then_inc(q["kv_free"], 1)
                    n += 1
                    for item in between.get(j, []) if part == 1 else []:
                        take_aux(item)
                for item in pre[j]:
                    take_aux(item)

            dve.wait_ge(q["proj_done"], 1)
            for s in range(NT + LAG):
                h, t = s // KT, s % KT
                if s < NT and on_dve(s):
                    dve.wait_ge(q["exp_ok"], s + 1)
                    if s >= NP:
                        dve.wait_ge(q["pv_ok"], s - LAG)
                    dve.tensor_tensor(PL[s % NP][:], PR[s % 3][:], PH[s % NP][:].bitcast(F32),
                                      ALU.subtract).then_inc(q["pl_dve"], 1)
                for item in step_extra[s]:
                    if item[0] in ("mx", "pr"):
                        take_aux(item)
                for _ in range(deq_at(s)):
                    zero_unit()
            take_aux(("pr", KV - 1, 0))
            take_aux(("pr", KV - 1, 1))
            norm_rows(1)
            take_nT(1)
            while units[unit][0] == "down":
                zero_unit()
            dve.memset(dt_t[R:R + 1, :], 1.0).then_inc(q["dt_one"], 1)
            for p in range(DT // 2 + 1):
                if p < DT // 2:
                    dve.wait_ge(q["conv_a"], p + 1)
                    former = seq[0]
                    for shift in range(1, TAPS):
                        for i in (2 * p, 2 * p + 1):
                            if shift > 1:
                                former += 1
                                dve.wait_ge(q["dve_seq"], former)
                            src = u_bank(i)
                            tap = dve.scalar_tensor_tensor(
                                u_c[:, i, shift:T], src[:, (i % 2) * T:(i % 2 + 1) * T - shift],
                                conv_w[:, i, TAPS - 1 - shift:TAPS - shift], u_c[:, i, shift:T], ALU.mult, ALU.add)
                            if shift < TAPS - 1:
                                tap.then_inc(q["dve_seq"], 1)
                                seq[0] += 1
                            else:
                                tap.then_inc(q["conv_ok"], 1)
                if p >= 1:
                    sl = slice(2 * p - 2, 2 * p)
                    dve.wait_ge(q["sil_a"], p)
                    dve.tensor_tensor(u_c[:, sl, :], u_c[:, sl, :], sig[:, sl, :], ALU.mult).then_inc(q["u_ok"], 1)
                if p == 1:
                    zero_unit()
            zero_unit()
            zero_unit()
            dve.wait_ge(q["rms_ok"], 1)
            for a, (lo, hi) in enumerate(DT_B_C):
                dve.scalar_tensor_tensor(sp[:, lo:hi], banks[4][:, lo:hi], norm[:, 2 + a:3 + a], ln_b[:, lo:hi],
                                         ALU.mult, ALU.mult).then_inc(q["spn_ok"], 1)
            dve.wait_ge(q["spn_ok"], 3)
            chain(dve.tensor_copy(sp_h[:], sp[:, R:]))
            dve.tensor_tensor(sp_l[:], sp[:, R:], sp_h[:].bitcast(F32), ALU.subtract).then_inc(q["bc_split"], 1)
            zero_unit()
            zero_unit()
            sl = slice(DT // 2, DT)
            dve.wait_ge(q["delta_filled"], 2)
            z = banks[7][:, :].rearrange("p (i t) -> p i t", i=4)
            dve.tensor_scalar(sig[:, sl, :], z, -1.0, None, ALU.mult).then_inc(q["neg_ok"], 1)
            dve.wait_ge(q["neg_ok"], 1)
            dve.tensor_tensor(sig[:, sl, :], sig[:, sl, :], z, ALU.min).then_inc(q["nabs_ok"], 1)
            zero_unit()
            take_bcast(0)
            for half in range(2):
                sl = slice(4 * half, 4 * half + 4)
                dve.wait_ge(q["dl_a"], half + 1)
                z = banks[6 + half][:, :].rearrange("p (i t) -> p i t", i=4)
                dve.scalar_tensor_tensor(delta[:, sl, :], z, 0.0, sig[:, sl, :], ALU.max, ALU.add).then_inc(q["delta_ok"], 1)
                dve.wait_ge(q["delta_ok"], half + 1)
                dve.tensor_tensor(du[:, sl, :], delta[:, sl, :], u_c[:, sl, :], ALU.mult).then_inc(q["du_ok"], 1)
            dve.wait_ge(q["bb_act"], 1)
            dve.wait_ge(q["bb_dve"], 1)
            dve.wait_ge(q["du_ok"], 1)
            for half in range(2):
                if half == 1:
                    take_bcast(2)
                    take_bcast(3)
                    dve.wait_ge(q["bb_dve"], 3)
                n = slice(half * N // 2, (half + 1) * N // 2)
                dve.tensor_tensor(dBu[0][:, n, :], B_b[:, n, :], du[:, 0:1, :].to_broadcast([P, N // 2, T]),
                                  ALU.mult).then_inc(q["dBu_dve"], 1)

            def gate_out(i):
                dve.wait_ge(q["y_filled"], i + 1)
                if i >= 2:
                    dve.wait_ge(q["y2_used"], i - 1)
                dve.tensor_tensor(y2[i % 2][:], banks[6 + i % 2][:, 0:T], g_s[:, i, :], ALU.mult).then_inc(q["y2_ok"], 1)

            def scan(i, part, parts):
                n = slice(part * N // parts, (part + 1) * N // parts)
                flat = dBu[i % 3][:, n, :].rearrange("p n t -> p (n t)")
                dve.wait_ge(q["dA_ok"], 2 * i + 2 * (part + 1) // parts)
                dve.tensor_tensor_scan(flat, dA[i % 2][:, n, :].rearrange("p n t -> p (n t)"), flat, 0.0,
                                       ALU.mult, ALU.add).then_inc(q["scan_ok"], 1)

            def times_c(i, part, parts):
                n = slice(part * N // parts, (part + 1) * N // parts)
                dve.wait_ge(q["scan_ok"], parts_before(i) + part + 1)
                dve.tensor_tensor(dBu[i % 3][:, n, :], dBu[i % 3][:, n, :], C_b[:, n, :], ALU.mult).then_inc(q["yc_ok"], 1)

            dve.wait_ge(q["dBu_dve"], 1)
            scan(0, 0, 2)
            take_bcast(4)
            dve.wait_ge(q["dBu_dve"], 2)
            scan(0, 1, 2)
            take_bcast(5)
            dve.wait_ge(q["bb_dve"], 5)
            times_c(0, 0, 2)
            dve.wait_ge(q["bb_act"], 3)
            times_c(0, 1, 2)
            gate(0)
            for i in range(1, DT - 1):
                dve.wait_ge(q["dBu_pool"], i)
                scan(i, 0, 1)
                if i == 1:
                    gate(1)
                    dve.wait_ge(q["gs_ok"], 2)
                if i >= 2:
                    gate_out(i - 2)
                times_c(i, 0, 1 if i < DT - 2 else 2)
            dve.wait_ge(q["dBu_pool"], DT - 1)
            for part in range(2):
                scan(DT - 1, part, 2)
                gate_out(DT - 3 + part)
                times_c(DT - 1, part, 2)
            gate_out(DT - 1)
            dve.wait_ge(q["y2_used"], DT)
            chain(dve.tensor_tensor(x_res[:], banks[2][:, :], x_res[:], ALU.add))
            norm_rows(2)
            take_nT(2)
            while unit < len(units):
                zero_unit()
            for m in range(ffn_groups()):
                n = min(GI, IT - GI * m) * T
                dve.wait_ge(q["fs_a"], m + 1)
                hs = h_T[:, GI * m:GI * m + n // T, :].rearrange("p i t -> p (i t)")
                chain(dve.tensor_tensor(f_sig[m % 2][:, 0:n], banks[2 * (m % 2)][:, 0:n], f_sig[m % 2][:, 0:n], ALU.mult))
                dve.tensor_tensor(hs, banks[2 * (m % 2) + 1][:, 0:n], f_sig[m % 2][:, 0:n],
                                  ALU.mult).then_inc(q["h_part"], 1)
                if GI * m < SPLIT:
                    g = slice(GI * m, GI * m + GI)
                    dve.wait_ge(q["h_high"], m + 1)
                    dve.tensor_tensor(h_L[:, g, :], h_T[:, g, :], h_H[:, g, :].bitcast(F32),
                                      ALU.subtract).then_inc(q["h_low"], 1)
            dve.wait_ge(q["down_filled"], 1)
            dve.tensor_tensor(y_out[:], banks[5][:, :], x_res[:], ALU.add).then_inc(q["fin_ok"], 1)

        @block.tensor
        def _(pe):
            def mm3(dst, wh, wl, xh, xl, start, stop):
                pe.matmul(dst, wh, xh, start=start, stop=False)
                pe.matmul(dst, wh, xl, start=False, stop=False)
                return pe.matmul(dst, wl, xh, start=False, stop=stop)

            def start_aux(item):
                pair, k = aux_of(item)
                if k >= 1:
                    pe.wait_ge(aux_free[pair], k)
                a, b = aux[pair]
                if item[0] == "xT":
                    pe.wait_ge(q["consts"], 1)
                    for k4 in range(KD):
                        pe.wait_ge(q["xn_ok"], 1 + k4 // 2)
                        last = pe.transpose(a[:, k4 * T:(k4 + 1) * T], x_n[:, k4 * P:(k4 + 1) * P], ident[:])
                elif item[0] == "q":
                    h = item[1]
                    pe.wait_ge(q["xT_copy"], 1)
                    pe.wait_ge(q[f"wq_in{h % 2}"], 16 * (h // 2 + 1))
                    for g in range(G):
                        for k4 in range(KD):
                            last = pe.matmul(a[0:HD, g * T:(g + 1) * T], w_raw[h % 2][:, k4, g * HD:(g + 1) * HD],
                                             x_nT[:, k4, :], start=(k4 == 0), stop=(k4 == KD - 1))
                elif item[0] == "mx":
                    _, h, j = item
                    lo, hi = chunk_cols(j)
                    if h == 0:
                        pe.wait_ge(q["kv_high"], kv_items_upto(j - 1) + 1)
                    pe.wait_ge(q["q_high"], h + 1)
                    for g in range(G):
                        bk = (a, b)[g // 2]
                        w = hi - lo
                        last = pe.matmul(bk[:, (g % 2) * w:(g % 2 + 1) * w], QH[0:HD, h, g * T:(g + 1) * T],
                                         KH[0:HD, h, lo:hi], start=True, stop=True)
                elif item[0] == "nm":
                    h = item[1]
                    pe.wait_ge(q["max_ok"], h + 1)
                    pe.wait_ge(q["ident_ok"], 1)
                    for g in range(G):
                        c = G * h + g
                        last = pe.matmul(a[0:HK, g * T:(g + 1) * T], neg_max[:, c:c + HK], ident_r[:],
                                         start=True, stop=True)
                elif item[0] == "pr":
                    _, h, half = item
                    if half == 0:
                        pe.wait_ge(q["o_raw_ok"], h + 1)
                        pe.wait_ge(q[f"wo_in{h % 2}"], 16 * (h // 2 + 1))
                        if h >= 1:
                            pe.wait_ge(q["recip_ok"], h)
                        for g in range(G):
                            last = pe.matmul(banks[3][:, g:g + 1], o_raw[HD:HK, g * T:(g + 1) * T], one[HD:HK, :],
                                             start=True, stop=True)
                        last.then_inc(q["sums_filled"], 1)
                    for m, bk in enumerate((a, b)):
                        g = 2 * half + m
                        last = pe.matmul(bk[:, :], o_raw[0:HD, g * T:(g + 1) * T], WO[h % 2][:, g, :],
                                         start=True, stop=True)
                last.then_inc(aux_filled[pair], 1)
                if item[0] == "q" and item[1] + 2 < KV:
                    pe.wait_ge(aux_filled[pair], aux_of(item)[1] + 1)
                    pe.sem_inc(q["wq_free"], 1)

            start_aux(("xT",))
            n = 0
            for j in range(NCH):
                lo, hi = chunk_cols(j)
                w = hi - lo
                hh, hl = HH[j % 2], HL[j % 2]
                if j == 0:
                    pe.wait_ge(q["tail_low"], 1)
                else:
                    pe.wait_ge(q["ctx_split"], 2 * j)
                for part in range(kv_parts(j)):
                    if n >= 4:
                        pe.wait_ge(q["kv_free"], n - 3)
                    dst = banks[n % 4]
                    if part < 2:
                        for m in range(2 - part):
                            c = slice((2 * part + m) * P, (2 * part + m + 1) * P)
                            for k4 in range(KD):
                                if j == 0:
                                    pe.wait_ge(q["wk_split"], 1 + k4 // 2)
                                last = mm3(dst[:, m * w:(m + 1) * w], WKH[:, k4, c], WKL[:, k4, c],
                                           hh[:, k4, 0:w], hl[:, k4, 0:w], k4 == 0, k4 == KD - 1)
                    else:
                        if n == 2:
                            pe.wait_ge(q["wv_split"], 1)
                        c = slice((part - 2) * P, (part - 1) * P)
                        for k4 in range(KD):
                            last = mm3(dst[:, 0:KV * HD], hh[:, k4, c], hl[:, k4, c],
                                       WVH[:, k4, :], WVL[:, k4, :], k4 == 0, k4 == KD - 1)
                    last.then_inc(q["kv_filled"], 1)
                    n += 1
                    for item in between.get(j, []) if part == 1 else []:
                        start_aux(item)
                for item in pre[j]:
                    start_aux(item)
                    if j == NCH - 1 and item[0] == "q":
                        pair, k = aux_of(item)
                        pe.wait_ge(aux_filled[pair], k + 1)
                        pe.sem_inc(q["proj_done"], 1)
            pe.wait_ge(q["kv_free"], n)
            pe.wait_ge(q["pads"], 5)

            for s in range(NT + LAG):
                h, t = s // KT, s % KT
                if s < NT:
                    if t == 0:
                        pair, k = aux_of(("nm", h))
                        pe.wait_ge(aux_free[pair], k + 1)
                    if s >= 2:
                        pe.wait_ge(q["exp_ok"], s - 1)
                    kc = slice(t * P, (t + 1) * P)
                    mm3(banks[s % 2][:, :], KH[:, h, kc], KL[:, h, kc], QH[:, h, :], QL[:, h, :],
                        True, True).then_inc(q["s_filled"], 1)
                for item in step_extra[s]:
                    start_aux(item)
                v = s - LAG
                if 0 <= v < NT:
                    hd, t = v // KT, v % KT
                    pe.wait_ge(*low_part(v))
                    if t == 0 and hd >= 1:
                        pe.wait_ge(q["o_raw_ok"], hd)
                    last = mm3(banks[2][0:HK, :], VH[:, hd, t, 0:HK], VL[:, hd, t, 0:HK],
                               PH[v % NP][:], PL[v % NP][:], t == 0, t == KT - 1)
                    last.then_inc(q["pv_ok"], 1)
                    if t == KT - 1:
                        pe.wait_ge(q["pv_ok"], v + 1)
                        pe.sem_inc(q["head_done"], 1)
            start_aux(("pr", KV - 1, 0))
            start_aux(("pr", KV - 1, 1))

            def transposes(k):
                for k4 in range(KD):
                    pe.wait_ge(q["xn_ok"], 2 * k + 1 + k4 // 2)
                    last = pe.transpose(banks[4 + k4 // 2][:, k4 % 2 * T:(k4 % 2 + 1) * T],
                                        x_n[:, k4 * P:(k4 + 1) * P], ident[:])
                    if k4 % 2 == 1:
                        last.then_inc(q["nT_filled"], 1)

            def half_ready(k, k4):
                pe.wait_ge(q[("nT_act", "nT_dve")[k4 // 2]], k)

            transposes(1)
            pe.wait_ge(q["winu_in"], 16)
            for i in range(DT):
                for k4 in range(KD):
                    if i == 0:
                        half_ready(1, k4)
                    last = pe.matmul(u_bank(i)[:, (i % 2) * T:(i % 2 + 1) * T], w_inu[:, k4, i * P:(i + 1) * P],
                                     x_T[:, k4, :], start=(k4 == 0), stop=(k4 == KD - 1))
                if i % 2 == 1:
                    last.then_inc(q["u_filled"], 1)
            pe.wait_ge(q["wing_in"], 16)
            pe.wait_ge(q["wx_in"], 48)
            for i in range(DT):
                for k4 in range(KD):
                    last = pe.matmul(banks[2 + i // 4][:, (i % 4) * T:(i % 4 + 1) * T], w_ing[:, k4, i * P:(i + 1) * P],
                                     x_T[:, k4, :], start=(k4 == 0), stop=(k4 == KD - 1))
                if i % 4 == 3:
                    last.then_inc(q["g_filled"], 1)
                for p in {2: (0,), 3: (1,), 4: (2, 3)}.get(i, ()):
                    pe.wait_ge(q["u_ok"], p + 1)
                    for m in (2 * p, 2 * p + 1):
                        last = pe.matmul(banks[4][:, 0:R + 2 * N], u_c[:, m, :], w_x[:, m, :],
                                         start=(m == 0), stop=(m == DT - 1))
                    if p == 3:
                        last.then_inc(q["ssm_filled"], 1)
            pe.wait_ge(q["spn_ok"], 1)
            pe.transpose(banks[5][0:R, 0:T], sp[:, 0:R], ident[:]).then_inc(q["tr_filled"], 1)

            def broadcast(k):
                if k >= 4:
                    pe.wait_ge(*((q["bb_act"], 1) if k == 5 else (q["bb_dve"], (1, 1, 2, 3)[k - 4])))
                for m in range(4):
                    n = 4 * k + m
                    dst = banks[(0, 1, 4, 5)[k % 4]][:, m * T:(m + 1) * T]
                    pe.matmul(dst, sp_h[:, n:n + 1].to_broadcast([P, P]), ident_r[:], start=True, stop=False)
                    last = pe.matmul(dst, sp_l[:, n:n + 1].to_broadcast([P, P]), ident_r[:], start=False, stop=True)
                last.then_inc(q["bb_filled"], 1)

            pe.wait_ge(q["dt_ok"], 1)
            pe.wait_ge(q["dt_one"], 1)
            for i in range(DT):
                last = pe.matmul(banks[6 + i // 4][:, (i % 4) * T:(i % 4 + 1) * T], w_dt[:, i * P:(i + 1) * P],
                                 dt_t[:], start=True, stop=True)
                if i % 4 == 3:
                    last.then_inc(q["delta_filled"], 1)
            pe.wait_ge(q["ident_ok"], 1)
            pe.wait_ge(q["bc_split"], 1)
            for k in range(8):
                broadcast(k)

            def mamba_out(i):
                pe.wait_ge(q["y2_ok"], i + 1)
                if i == 0:
                    pe.wait_ge(q["gs_ok"], 2)
                    pe.wait_ge(q["wout_in"], 16)
                last = pe.matmul(banks[2][:, :], y2[i % 2][:], w_out[:, i, :], start=(i == 0), stop=(i == DT - 1))
                last.then_inc(q["y2_used"], 1)

            pe.wait_ge(q["delta_ok"], 2)
            pe.wait_ge(q["diag_ok"], 1)
            for i in range(DT):
                if i >= 2:
                    pe.wait_ge(q["y2_ok"], i - 1)
                pe.matmul(banks[6 + i % 2][:, 0:T], d_diag[:, i, :], u_c[:, i, :], start=True, stop=False)
                pe.wait_ge(q["yc_ok"], parts_before(i) + 1)
                for m in range(N):
                    if m == N // 2 and i in (0, DT - 1):
                        pe.wait_ge(q["yc_ok"], parts_before(i) + 2)
                    elif m == N // 2 and i == DT - 2:
                        pe.wait_ge(q["yc_pool"], 1)
                    last = pe.matmul(banks[6 + i % 2][:, 0:T], ident[:], dBu[i % 3][:, m, :],
                                     start=False, stop=(m == N - 1))
                last.then_inc(q["y_filled"], 1)
                if i >= 1:
                    mamba_out(i - 1)
            mamba_out(DT - 1)
            def down(m):
                for i in range(GI * m, min(GI * m + GI, IT)):
                    first, last = i == 0, i == IT - 1
                    if i < SPLIT:
                        pe.wait_ge(q["wdn_low"], i + 1)
                        pe.wait_ge(q["h_low"], m + 1)
                        mm = mm3(banks[5][:, :], h_H[:, i, :], h_L[:, i, :], w_dnH[:, i, :], w_dnL[:, i, :], first, last)
                    else:
                        pe.wait_ge(*scaled(units.index(("down", i, 0))))
                        pe.wait_ge(q["h_part"], m + 1)
                        w = w_dn[:, i, :] if i < IT - 1 else w_dnx[:, 0, :]
                        mm = pe.matmul(banks[5][:, :], h_T[:, i, :], w, start=first, stop=last)
                if m == ffn_groups() - 1:
                    mm.then_inc(q["down_filled"], 1)

            transposes(2)
            for m in range(ffn_groups()):
                if m >= 2:
                    pe.wait_ge(q["h_part"], m - 1)
                for side, (w, kind) in enumerate(((w_gate, "gate"), (w_up, "up"))):
                    pe.wait_ge(*scaled(units.index((kind, KD - 1, (min(GI * m + GI, IT) * P - 1) // ZC))))
                    for c in range(min(GI, IT - GI * m)):
                        i = GI * m + c
                        for k4 in range(KD):
                            if m == side == c == 0:
                                half_ready(2, k4)
                            last = pe.matmul(banks[2 * (m % 2) + side][:, c * T:(c + 1) * T],
                                             w[:, k4, i * P:(i + 1) * P], x_T[:, k4, :],
                                             start=(k4 == 0), stop=(k4 == KD - 1))
                last.then_inc(q["gu_filled"], 1)
                if m >= 2:
                    down(m - 2)
            for m in range(ffn_groups() - 2, ffn_groups()):
                down(m)


def ffn_groups():
    return (IT + GI - 1) // GI


def kv_parts(j):
    return 3 if j == 0 else 2 + CH // P


def key_moves(dst, src, part, lo, hi):
    w = hi - lo
    if part == 0:
        moves = [(dst[0:HD, 0:2, lo:hi], src[0:HD, 0:2 * w].rearrange("p (h t) -> p h t", h=2))]
    else:
        moves = [(dst[0:HD, 2, lo:hi], src[0:HD, 0:w])]
    third = HD // (KV - 1)
    for m in range(2 - part):
        tile = 2 * part + m
        moves.append((dst[tile * third:(tile + 1) * third, KV - 1, lo:hi], src[HD:P, m * w:(m + 1) * w]))
    return moves


def kv_items_upto(j):
    return sum(kv_parts(i) for i in range(j + 1))


def down_tiles(h):
    lo = (h * KT * VW) // D
    hi = ((h + 1) * KT * VW) // D
    return lo, (IT if h == KV - 1 else hi)


def units_of(h):
    u = [(k, h, c) for k in ("gate", "up") for c in range(I // ZC)]
    lo, hi = down_tiles(h)
    return u + [("down", i, 0) for i in range(lo, hi)]


def kernel(**inputs):
    import numpy as np
    import concourse.bacc as bacc
    from concourse.bass_utils import run_bass_kernel_spmd

    def rows(a, parts=P):
        return np.ascontiguousarray(a.reshape(-1, parts, a.shape[-1]).transpose(1, 0, 2))

    v = {k: np.asarray(a) for k, a in inputs.items()}
    m = {k[8:] if k.startswith("L0_attn_") else k: a for k, a in v.items()}
    third = HD // (KV - 1)
    k_rows = [r for h in range(KV - 1) for r in (*range(h * HD, (h + 1) * HD),
                                                 *range((KV - 1) * HD + h * third, (KV - 1) * HD + (h + 1) * third))]
    data = {
        "x": v["x"][0],
        "ctx": rows(v["ctx_4096"][0].T),
        "wq": rows(v["L0_xattn_Wq"].T),
        "wk": rows(v["L0_xattn_Wk"][k_rows].T),
        "wv": rows(v["L0_xattn_Wv"].T),
        "wo": rows(v["L0_xattn_Wo"].T, HD),
        "w_in": rows(m["W_in"].T),
        "conv_w": rows(m["conv_w"]),
        "conv_b": m["conv_b"].reshape(DT, P).T,
        "a": rows(m["A"]),
        "d": m["D_param"].reshape(DT, P).T,
        "ln_dt": m["dt_ln_w"].reshape(1, R),
        "ln_b": m["b_ln_w"].reshape(1, N),
        "ln_c": m["c_ln_w"].reshape(1, N),
        "w_x": rows(m["Wx"].T),
        "w_dt": m["Wdt"].T,
        "dt_bias": m["dt_bias"].reshape(1, DI),
        "w_out": rows(m["W_out"].T),
        "gate_w": rows(v["L0_ffn_gate_w"]),
        "up_w": rows(v["L0_ffn_up_w"]),
        "down_w": rows(v["L0_ffn_down_w"]),
        "gate_z": v["L0_ffn_gate_z"], "gate_s": v["L0_ffn_gate_s"],
        "up_z": v["L0_ffn_up_z"], "up_s": v["L0_ffn_up_s"],
        "down_z": v["L0_ffn_down_z"], "down_s": v["L0_ffn_down_s"],
    }
    nc = bacc.Bacc("TRN2", target_bir_lowering=False, num_devices=1)
    arrays, aps = {}, {}
    for name, a in data.items():
        a = np.ascontiguousarray(a)
        arrays["in_" + name] = a
        aps[name] = nc.dram_tensor("in_" + name, a.shape, mybir.dt.from_np(a.dtype), kind="ExternalInput").ap()
    out = nc.dram_tensor("y", (T, D), F32, kind="ExternalOutput").ap()
    build(nc, aps, out)
    r = run_bass_kernel_spmd(nc, [arrays], core_ids=[0])
    return r.results[0]["y"].reshape(1, T, D)
```
